# Optimizing a Trainium2 kernel written in Bass

```python
import numpy as np
import jax
import jax.numpy as jnp

def _softmax(x, axis=-1):
    return jax.nn.softmax(x, axis=axis)

def _gelu(x):
    return jax.nn.gelu(x, approximate=True)

def _silu(x):
    return jax.nn.silu(x)

def _sigmoid(x):
    return jax.nn.sigmoid(x)

def _layernorm(x, axis=-1, eps=1e-05):
    m = jnp.mean(x, axis=axis, keepdims=True)
    v = jnp.var(x, axis=axis, keepdims=True)
    return (x - m) / jnp.sqrt(v + eps)

def _scatter_add(tgt, idx, src, axis=0):
    return tgt.at[idx].add(src)

def _segment_sum(src, seg, n):
    return jax.ops.segment_sum(src, seg, n)
kernel_name = 'mk_flamingo_gated_d1_seqx_r4_fc5414'

def setup_inputs(seed: int=0):
    np.random.seed(seed)
    _w = jnp.asarray

    def _rec_inputs():
        import jax
        import jax.numpy as jnp
        _rk = jax.random.key(seed)
        x = -0.0003929 + 0.9999 * jax.random.normal(jax.random.fold_in(_rk, 1), (4, 512, 256), jnp.float32)
        _lenS = 512 - jax.random.randint(jax.random.fold_in(_rk, 7), (4,), 0, max(1, 512 // 4) + 1, jnp.int32)
        _lenS2 = 1601 - jax.random.randint(jax.random.fold_in(_rk, 8), (4,), 0, max(1, 1601 // 4) + 1, jnp.int32)
        _ctx_1024P = jax.random.normal(jax.random.fold_in(_rk, 11), (4, 16, 256), jnp.float32)
        _ctx_1024c = jax.random.dirichlet(jax.random.fold_in(_rk, 511), 0.3 * jnp.ones((16,), jnp.float32), (4, 1601))
        _ctx_1024t = jnp.einsum('bsk,bkd->bsd', _ctx_1024c, _ctx_1024P)
        _ctx_1024t = _ctx_1024t * jax.lax.rsqrt(jnp.mean(jnp.square(_ctx_1024t)) + 1e-12) * 0.953939
        ctx_1024 = 2.81802e-05 + 1.00001 * (_ctx_1024t + 0.3 * jax.random.normal(jax.random.fold_in(_rk, 611), (4, 1601, 256), jnp.float32))
        _validS = jnp.arange(512)[None, :] < _lenS[:, None]
        _validS2 = jnp.arange(1601)[None, :] < _lenS2[:, None]
        _causal = jnp.tril(jnp.ones((512, 512), dtype=bool))
        mask_SxS2_ik0 = jnp.where(jnp.broadcast_to(_validS2[0:1, :], (512, 1601)), 0, 1).astype(jnp.int32)
        _g = jax.random.normal(jax.random.fold_in(_rk, 9001), (2, 1), jnp.float32)
        _g = jnp.sign(_g) * jnp.maximum(jnp.abs(_g), 1.0) + (_g == 0) * 1.0
        g_xattn = _g[0]
        g_ffn = _g[1]
        return (x, ctx_1024, mask_SxS2_ik0, g_xattn, g_ffn)
    x, ctx_1024, mask_SxS2_ik0, g_xattn, g_ffn = _rec_inputs()

    def _L0_xattn_setup():
        import jax, jax.numpy as jnp
        import numpy as np
        B, S, D = (4, 1024, 256)
        NUM_Q_HEADS = 16
        D_K = D // NUM_Q_HEADS
        INIT_SCALE = 0.02
        key = jax.random.key(seed)
        ks = jax.random.split(key, 11)
        s = INIT_SCALE
        return {'Q': jax.random.normal(ks[0], (B, S, D), dtype=jnp.float32), 'K': jax.random.normal(ks[1], (B, S, D), dtype=jnp.float32), 'V': jax.random.normal(ks[2], (B, S, D), dtype=jnp.float32), 'Wq': jax.random.normal(ks[3], (D, D), dtype=jnp.float32) * s, 'bq': jnp.zeros((D,), jnp.float32), 'Wk': jax.random.normal(ks[4], (D, D), dtype=jnp.float32) * s, 'bk': jnp.zeros((D,), jnp.float32), 'Wv': jax.random.normal(ks[5], (D, D), dtype=jnp.float32) * s, 'bv': jnp.zeros((D,), jnp.float32), 'Wo': jax.random.normal(ks[6], (D, D), dtype=jnp.float32) * s, 'bo': jnp.zeros((D,), jnp.float32), 'mask': jnp.tril(jnp.ones((S, S), dtype=jnp.int32))}
    _L0_xattn_all = _L0_xattn_setup()
    _L0_xattn_in = {k: v for k, v in _L0_xattn_all.items() if k in ('Wq', 'bq', 'Wk', 'bk', 'Wv', 'bv', 'Wo', 'bo')}
    del _L0_xattn_all

    def _L0_ffn_setup():
        import jax, jax.numpy as jnp
        import numpy as np
        EMB = 256
        FF = 4 * EMB

        def _ternary(w):
            scale = jnp.maximum(jnp.mean(jnp.abs(w)), 1e-08)
            w_t = jnp.clip(jnp.round(w / scale), -1.0, 1.0)
            return w + jax.lax.stop_gradient(w_t - w)
        key = jax.random.key(seed)
        kx, k1, k2, kb1, kb2 = jax.random.split(key, 5)
        x = jax.random.normal(kx, (4, 512, EMB), dtype=jnp.float32)
        lim1 = 1.0 / np.sqrt(EMB)
        lim2 = 1.0 / np.sqrt(FF)
        W1 = jax.random.uniform(k1, (FF, EMB), jnp.float32, -lim1, lim1)
        b1 = jax.random.uniform(kb1, (FF,), jnp.float32, -lim1, lim1)
        W2 = jax.random.uniform(k2, (EMB, FF), jnp.float32, -lim2, lim2)
        b2 = jax.random.uniform(kb2, (EMB,), jnp.float32, -lim2, lim2)
        return {'x': x, 'W1': W1, 'b1': b1, 'W2': W2, 'b2': b2}
    _L0_ffn_all = _L0_ffn_setup()
    _L0_ffn_in = {k: v for k, v in _L0_ffn_all.items() if k in ('W1', 'b1', 'W2', 'b2')}
    del _L0_ffn_all
    return {'x': x, 'ctx_1024': ctx_1024, 'mask_SxS2_ik0': mask_SxS2_ik0, 'g_xattn': g_xattn, 'g_ffn': g_ffn, 'L0_xattn_Wq': _L0_xattn_in['Wq'], 'L0_xattn_bq': _L0_xattn_in['bq'], 'L0_xattn_Wk': _L0_xattn_in['Wk'], 'L0_xattn_bk': _L0_xattn_in['bk'], 'L0_xattn_Wv': _L0_xattn_in['Wv'], 'L0_xattn_bv': _L0_xattn_in['bv'], 'L0_xattn_Wo': _L0_xattn_in['Wo'], 'L0_xattn_bo': _L0_xattn_in['bo'], 'L0_ffn_W1': _L0_ffn_in['W1'], 'L0_ffn_b1': _L0_ffn_in['b1'], 'L0_ffn_W2': _L0_ffn_in['W2'], 'L0_ffn_b2': _L0_ffn_in['b2']}

def reference(x, ctx_1024, mask_SxS2_ik0, g_xattn, g_ffn, L0_xattn_Wq, L0_xattn_bq, L0_xattn_Wk, L0_xattn_bk, L0_xattn_Wv, L0_xattn_bv, L0_xattn_Wo, L0_xattn_bo, L0_ffn_W1, L0_ffn_b1, L0_ffn_W2, L0_ffn_b2):
    import jax
    import jax.numpy as jnp

    def _L0_xattn_ref(Q, K, V, Wq, bq, Wk, bk, Wv, bv, Wo, bo, mask):
        import jax, jax.numpy as jnp
        import numpy as np
        B, S, D = (4, 1024, 256)
        NUM_Q_HEADS = 16
        D_K = D // NUM_Q_HEADS
        INIT_SCALE = 0.02
        q = Q @ Wq + bq
        k = K @ Wk + bk
        v = V @ Wv + bv
        scale = 1.0 / np.sqrt(D_K).astype(np.float32)
        scores = jnp.einsum('bqd,bkd->bqk', q, k) * scale
        scores = jnp.where(mask == 0, jnp.asarray(-1000000000.0, scores.dtype), scores)
        probs = jax.nn.softmax(scores, axis=-1)
        attn = jnp.einsum('bqk,bkd->bqd', probs, v)
        return attn @ Wo + bo

    def _L0_ffn_ref(x, W1, b1, W2, b2):
        import jax, jax.numpy as jnp
        import numpy as np
        EMB = 256
        FF = 4 * EMB

        def _ternary(w):
            scale = jnp.maximum(jnp.mean(jnp.abs(w)), 1e-08)
            w_t = jnp.clip(jnp.round(w / scale), -1.0, 1.0)
            return w + jax.lax.stop_gradient(w_t - w)
        h = jnp.einsum('bsd,fd->bsf', x, _ternary(W1)) + b1
        h = jax.nn.gelu(h, approximate=False)
        out = jnp.einsum('bsf,df->bsd', h, _ternary(W2)) + b2
        return out
    x = x + jnp.tanh(g_xattn[0]) * _L0_xattn_ref(_layernorm(x, axis=-1), ctx_1024, ctx_1024, L0_xattn_Wq, L0_xattn_bq, L0_xattn_Wk, L0_xattn_bk, L0_xattn_Wv, L0_xattn_bv, L0_xattn_Wo, L0_xattn_bo, mask_SxS2_ik0)
    x = x + jnp.tanh(g_ffn[0]) * _L0_ffn_ref(_layernorm(x, axis=-1), L0_ffn_W1, L0_ffn_b1, L0_ffn_W2, L0_ffn_b2)
    return x

_drawn_inputs = setup_inputs


def setup_inputs(seed=0):
    import zlib

    import numpy as np

    out = dict(_drawn_inputs(seed))
    spreads = {'L0_xattn_bq': (0.0, 0.8),
     'L0_xattn_bk': (0.0, 2.0),
     'L0_xattn_bv': (0.0, 0.334),
     'L0_xattn_bo': (0.0, 0.1)}
    factors = {'L0_xattn_Wq': 8.0, 'L0_xattn_Wk': 8.0, 'L0_ffn_b1': 24.854, 'L0_ffn_b2': 64.0}
    for name, (base, spread) in spreads.items():
        noise = np.random.default_rng([zlib.crc32(name.encode()), seed]).standard_normal(out[name].shape)
        drawn = base * np.exp(spread * noise) if base else spread * noise
        out[name] = jnp.asarray(drawn.astype(out[name].dtype))
    for name, factor in factors.items():
        out[name] = (out[name] * factor).astype(out[name].dtype)
    return out
```

```python
from contextlib import ExitStack

import concourse.bass as bass
from concourse import mybir

F32 = mybir.dt.float32
F32R = mybir.dt.float32r
BF16 = mybir.dt.bfloat16
I32 = mybir.dt.int32
ALU = mybir.AluOpType
ACT = mybir.ActivationFunctionType
AX = mybir.AxisListType

P = 128
BATCH, TOK, D = 4, 512, 256
KEYS = 1601
FF = 1024
TT = TOK // P
DC = D // P
KT = -(-KEYS // P)
KREM = KEYS - (KT - 1) * P
KEYS2 = KEYS + KEYS % 2
FT = FF // P
NCH = 4
CW = -(-KEYS2 // NCH)
CW += CW % 2
CSTART = [0] + [KEYS2 - (NCH - 1 - c) * (CW - 2) - (CW - 2) for c in range(1, NCH)]
CEND = CSTART[1:] + [KEYS2]
NS = TT * NCH
AHEAD = 6
HALF = 2 * 4 * P
EPS = 1e-5
SCALE = 0.25
MASKED = -float(2.0 ** 127)
RSQRT_SEED = 0x5F3759DF
EB = 2
SB = 4

PRO = (["X0", "X1", "WqT", "WkT", "M", "UC", "Q0", "Q1"] + [f"C{i}" for i in range(8)])
EXTRA_S = {6: ["WvT"], 7: ["Wvo"], 8: ["bvo"], 9: ["S1"], 13: ["A0", "A1"]}
EXTRA_K = {3: ["A2", "A3"], 6: ["S2"], 9: ["B0", "B1"], 12: ["B2", "B3"]}


def uses(first, last):
    plan = {"score": {}, "key": {}}
    for n in range(AHEAD, NS):
        u = [f"T{n - AHEAD}"]
        if first:
            u += EXTRA_S.get(n, [])
        if n == NS - 2 and not last:
            u.append("X0")
        if n == NS - 1 and not last:
            u.append("X1")
        plan["score"][n] = u
    plan["drain"] = (["T10", "T11", "T12", "T13"] if last
                     else ["T10", "Q0", "T11", "Q1", "T12", "T13"])
    for k in range(KT):
        u = []
        if k == 0:
            u.append("T14")
        if k == 1:
            u.append("T15")
        if 4 <= k < 12 and not last:
            u.append(f"C{k - 4}")
        if first:
            u += EXTRA_K.get(k, [])
        plan["key"][k] = u
    order = sum((plan["score"][n] for n in range(AHEAD, NS)), []) + plan["drain"]
    order += sum((plan["key"][k] for k in range(KT)), [])
    order += ["O0", "O1", "Y0", "Y1"] + [f"H{f}" for f in range(FT)]
    return plan, order


FIRST_PLAN, FIRST = uses(True, False)
MID_PLAN, MID = uses(False, False)
LAST_PLAN, LAST = uses(False, True)
NO_ACT = ("O", "W", "U", "b", "S", "A", "B")


def by_act(name):
    return name == "Wvo" or name[0] not in NO_ACT


class Batch:

    def __init__(self, b):
        self.b = b
        self.first = isinstance(b, int) and b == 0
        self.last = isinstance(b, int) and b == BATCH - 1
        self.plan, self.order = ((FIRST_PLAN, FIRST) if self.first else
                                 (LAST_PLAN, LAST) if self.last else (MID_PLAN, MID))

    def base(self, order_len, first_len, pro_len):
        if self.first:
            return pro_len
        return (self.b - 1) * order_len + (pro_len + first_len)

    def use(self, name):
        return self.base(len(MID), len(FIRST), len(PRO)) + self.order.index(name)

    def bank(self, name):
        at = 0 if self.first else len(FIRST)
        return (len(PRO) + at + self.order.index(name)) % EB

    def hi(self, name):
        n = [sum(map(by_act, o)) for o in (MID, FIRST, PRO)]
        return self.base(*n) + sum(map(by_act, self.order[:self.order.index(name)]))


assert len(MID) % EB == 0 and NS % SB == 0


def pro_hi(name):
    return sum(map(by_act, PRO[:PRO.index(name)]))


LN_STEPS = 2 + 3 + 3 * 3
ROW_STEPS = 2
GAIN_STEPS = 3
BODY_STEPS = 2 * LN_STEPS + ROW_STEPS + GAIN_STEPS


def build(nc, x, ctx_in, mask, g_x, g_f, Wq, bq, Wk, bk, Wv, bv, Wo, bo, W1, b1, W2, b2, out):
    with ExitStack() as stack:
        def sb(name, shape, dt):
            return stack.enter_context(nc.sbuf_tensor(name, shape, dt))

        def sem(name):
            return stack.enter_context(nc.semaphore(name))

        place = [(nc.sbuf_base + 31) // 32 * 32]

        def region(name, shape, dt):
            n = 1
            for s in shape[1:]:
                n *= s
            at = place[0]
            place[0] += (n * (2 if dt == BF16 else 4) + 31) // 32 * 32
            return nc.alloc_sbuf_tensor_at(name, shape, dt, offset=at), at

        def alias(name, shape, dt, at):
            return nc.alloc_sbuf_tensor_at(name, shape, dt, offset=at)

        pt_hi, _ = region("pt_hi", [P, KT, TOK], F32R)
        pt_lo, _ = region("pt_lo", [P, KT, TOK], F32R)
        c_hi, c_at = region("c_hi", [P, KT, D], F32R)
        c_lo, _ = region("c_lo", [P, KT, D], F32R)
        cT_hi, _ = region("cT_hi", [P, DC, KEYS2], F32R)
        cT_lo, _ = region("cT_lo", [P, DC, KEYS2], F32R)
        raw, _ = region("raw", [P, KT, D], F32)
        probs, _ = region("probs", [P, 2, KEYS], F32)
        mbias, _ = region("mbias", [P, TT, KEYS], BF16)
        qT_hi, _ = region("qT_hi", [P, DC, TOK], F32R)
        qT_lo, _ = region("qT_lo", [P, DC, TOK], F32R)
        xT_hi, _ = region("xT_hi", [P, DC, TOK], F32R)
        xT_lo, _ = region("xT_lo", [P, DC, TOK], F32R)
        xl, _ = region("xl", [P, TT, D], F32)
        xr, _ = region("xr", [P, TT, D], F32)
        hid, hid_at = region("hid", [P, 2, TOK], F32)
        xn2, _ = region("xn2", [P, TT, D], F32)
        w1T, w1T_at = region("w1T", [P, DC, FF], F32R)
        w2T, w2T_at = region("w2T", [P, FT, D], F32R)
        m_hi, _ = region("m_hi", [P, DC, D], F32R)
        m_lo, _ = region("m_lo", [P, DC, D], F32R)
        vo_hi, _ = region("vo_hi", [P, DC, D], F32R)
        vo_lo, _ = region("vo_lo", [P, DC, D], F32R)
        junk, _ = region("junk", [P, 2, D], BF16)
        U, _ = region("U", [P, D], F32)
        tb1, _ = region("tb1", [P, D], F32)
        tb2, _ = region("tb2", [P, D], F32)
        ident, _ = region("ident", [P, P], F32)
        tmp, _ = region("tmp", [P, 2 * TOK], F32)
        bqc, _ = region("bqc", [P, DC], F32)
        bkc, _ = region("bkc", [P, DC], F32)
        bvc, _ = region("bvc", [P, DC], F32)
        b1c, _ = region("b1c", [P, FT], F32)
        uc, _ = region("uc", [P, 3], F32)
        tg, _ = region("tg", [P, 2], F32)
        graw, _ = region("graw", [P, 2], F32)
        cmax, _ = region("cmax", [P, NCH], F32)
        nmax, _ = region("nmax", [P, TT], F32)
        sums, _ = region("sums", [P, TT, 2], F32)
        tot, _ = region("tot", [P, TT], F32)
        rec, _ = region("rec", [P, TT], F32)
        gain, _ = region("gain", [P, TT], F32)
        r_next, _ = region("r_next", [P, TT], F32)
        r_now, _ = region("r_now", [P, TT], F32)
        stats, _ = region("stats", [P, TT, 6], F32)
        mv, _ = region("mv", [P, TT, 2], F32)
        var, _ = region("var", [P, TT], F32)
        nhalf, _ = region("nhalf", [P, TT], F32)
        rs, _ = region("rs", [P, TT], F32)
        rt, _ = region("rt", [P, TT], F32)
        wsum, _ = region("wsum", [P, 1], F32)
        thr, _ = region("thr", [P, 2], F32)
        gate, _ = region("gate", [P, NS + 5], F32)
        pgate, _ = region("pgate", [P, 2], F32)
        ones, ones_at = region("ones", [P, P], F32)
        assert place[0] <= nc.sbuf_usable_end, place[0]
        mask_i = alias("mask_i", [P, TT, KEYS], I32, c_at)
        wraw = alias("wraw", [P, 4, DC, D], F32, w2T_at)
        wT = alias("wT", [P, 3, DC, D], F32, w1T_at)
        rep = alias("rep", [P, 2, DC, P], F32, w1T_at + 3 * DC * D * 4)
        w1raw = alias("w1raw", [P, FT, D], F32, hid_at)
        w2raw = alias("w2raw", [P, DC, FF], F32, hid_at)

        s_ps = [stack.enter_context(nc.psum_tensor(f"s_ps{i}", [P, 512], F32)) for i in range(SB)]
        e_ps = [stack.enter_context(nc.psum_tensor(f"e_ps{i}", [P, 512], F32)) for i in range(EB)]
        acc = [stack.enter_context(nc.psum_tensor(f"acc{i}", [P, 512], F32)) for i in range(2)]

        e_full, e_hi, e_free = sem("e_full"), sem("e_hi"), sem("e_free")
        s_full, s_biased, s_masked = sem("s_full"), sem("s_biased"), sem("s_masked")
        max_ready, exp_done = sem("max_ready"), sem("exp_done")
        pv_full, attn_hi, attn_split = sem("pv_full"), sem("attn_hi"), sem("attn_split")
        y_full, y_taken = sem("y_full"), sem("y_taken")
        xn_ready, xn2_ready, r_ready = sem("xn_ready"), sem("xn2_ready"), sem("r_ready")
        xl_loaded, xr_loaded, raw_loaded = sem("xl_loaded"), sem("xr_loaded"), sem("raw_loaded")
        xb_ready, x1b_ready = sem("xb_ready"), sem("x1b_ready")
        c_split, pool_step, dve_step = sem("c_split"), sem("pool_step"), sem("dve_step")
        qk_loaded, vo_loaded, bias_loaded = sem("qk_loaded"), sem("vo_loaded"), sem("bias_loaded")
        mask_loaded = [sem(f"mask_loaded{t}") for t in range(TT)]
        mask_ready = sem("mask_ready")
        w1_loaded, w2_loaded, gate_ready = sem("w1_loaded"), sem("w2_loaded"), sem("gate_ready")
        const_ready, ident_zero = sem("const_ready"), sem("ident_zero")
        tern_minus, tern_sum, tern = sem("tern_minus"), sem("tern_sum"), sem("tern")
        h_hi = sem("h_hi")
        wsum_ready, rep_ready = sem("wsum_ready"), sem("rep_ready")
        out_stored = sem("out_stored")

        xv = x.rearrange("b (t p) d -> b p t d", p=P)
        ov = out.rearrange("b (t p) d -> b p t d", p=P)
        cfull = ctx_in[:, 0:(KT - 1) * P, :].rearrange("b (t p) d -> b p t d", p=P)
        crem = ctx_in[:, (KT - 1) * P:KEYS, :]

        def of(ap, b, pat):
            return ap[bass.ds(b, 1)].rearrange(pat)

        def f32(ap):
            return ap.bitcast(F32)

        def weight_half(h):
            if h < 2:
                return w1raw[:, 4 * h:4 * h + 4, :], tmp[:].rearrange("p (f d) -> p f d", d=D)
            return (w2raw[:, :, (h - 2) * 512:(h - 1) * 512],
                    tmp[:].rearrange("p (c f) -> p c f", c=DC))

        block = stack.enter_context(nc.Block())

        @block.sync
        def _(sp):
            def load_x(dst, b, done):
                sp.dma_start(dst[:], of(xv, b, "b p t d -> (b p) t d")).then_inc(done, 16)

            def load_context(b):
                sp.dma_start(raw[:, 0:KT - 1, :],
                             of(cfull, b, "b p t d -> (b p) t d")).then_inc(raw_loaded, 16)
                sp.dma_start(raw[0:KREM, KT - 1, :],
                             of(crem, b, "b p d -> (b p) d")).then_inc(raw_loaded, 16)

            load_x(xl, 0, xl_loaded)
            for i, w in enumerate((Wq, Wk)):
                sp.dma_start(wraw[:, i, :, :], w.rearrange("(c p) n -> p c n", p=P)
                             ).then_inc(qk_loaded, 16)
            load_context(0)
            for t in range(TT):
                sp.dma_start(mask_i[:, t, :], mask[t * P:(t + 1) * P, :]
                             ).then_inc(mask_loaded[t], 16)
                if t == 1:
                    for i, w in ((2, Wv), (3, Wo)):
                        sp.dma_start(wraw[:, i, :, :], w.rearrange("(c p) n -> p c n", p=P)
                                     ).then_inc(vo_loaded, 16)
                    sp.dma_start(w1raw[:], W1.rearrange("(t p) d -> p t d", p=P)
                                 ).then_inc(w1_loaded, 16)

            def batch(b):
                at = Batch(b)
                if not at.last:
                    if at.first:
                        sp.wait_ge(r_ready, 1)
                        sp.wait_ge(e_full, PRO.index("X1") + 1)
                    else:
                        sp.wait_ge(e_full, at.base(len(MID), len(FIRST), len(PRO)))
                    load_x(xl, b + 1, xl_loaded)
                if not at.first:
                    sp.wait_ge(out_stored, b * (16 * 2))
                load_x(xr, b, xr_loaded)
                if at.first:
                    sp.wait_ge(tern, 2)
                    sp.dma_start(w2raw[:], W2.rearrange("(c p) f -> p c f", p=P)
                                 ).then_inc(w2_loaded, 16)
                if not at.last:
                    sp.wait_ge(c_split, b + 1)
                    if at.first:
                        sp.wait_ge(e_full, len(PRO))
                    load_context(b + 1)
                for h in range(2):
                    sp.wait_ge(y_taken, b * TT + 2 * h + 2)
                    sp.dma_start(of(ov, b, "b p t d -> (b p) t d")[:, 2 * h:2 * h + 2, :],
                                 xr[:, 2 * h:2 * h + 2, :]).then_inc(out_stored, 16)

            batch(0)
            with sp.Fori(1, BATCH - 1) as b:
                batch(b)
            batch(BATCH - 1)
            sp.wait_ge(out_stored, BATCH * 2 * 16)

        @block.gpsimd
        def _(pool):
            for dst, src in ((bqc, bq), (bkc, bk), (bvc, bv), (b1c, b1)):
                pool.dma_start(dst[:], src.rearrange("(c p) -> p c", p=P),
                               allow_slow_non_contiguous=True).then_inc(bias_loaded, 16)
            for i, g in enumerate((g_x, g_f)):
                pool.dma_start(graw[:, i:i + 1], g.partition_broadcast(P)).then_inc(bias_loaded, 16)
            for dst, src in ((tb1, bo), (tb2, b2)):
                pool.dma_start(dst[:], src.partition_broadcast(P)).then_inc(bias_loaded, 16)
            nc.gpsimd.memset(ident[:], 0.0).then_inc(ident_zero, 1)
            nc.gpsimd.memset(ones[:], 1.0).then_inc(const_ready, 1)
            nc.gpsimd.memset(pgate[:], 0.0).then_inc(const_ready, 1)
            nc.gpsimd.memset(f32(cT_hi[:, :, KEYS:KEYS2]), 0.0).then_inc(const_ready, 1)
            nc.gpsimd.memset(f32(cT_lo[:, :, KEYS:KEYS2]), 0.0).then_inc(const_ready, 1)
            pool.wait_ge(ident_zero, 1)
            nc.gpsimd.affine_select(out=ident[:], in_=ident[:], compare_op=ALU.not_equal, fill=1.0,
                                    base=0, pattern=[[-1, P]],
                                    channel_multiplier=1).then_inc(const_ready, 1)
            pool.wait_ge(const_ready, 5)

            def split_context(b):
                pool.wait_ge(raw_loaded, 32 * b + 32)
                if isinstance(b, int) and b == 0:
                    pool.wait_ge(mask_ready, TT)
                else:
                    pool.wait_ge(pv_full, b)
                nc.gpsimd.tensor_tensor(pgate[:, 0:1], pgate[:, 1:2], pgate[:, 1:2], ALU.add)
                for dst, a, z in ((P, 0, KT - 1), (KREM, KT - 1, KT)):
                    ins = nc.gpsimd.tensor_copy(c_hi[0:dst, a:z, :], raw[0:dst, a:z, :])
                ins.then_inc(pool_step, 1)
                pool.wait_ge(pool_step, b + 1)
                for dst, a, z in ((P, 0, KT - 1), (KREM, KT - 1, KT)):
                    ins = nc.gpsimd.tensor_tensor(c_lo[0:dst, a:z, :], raw[0:dst, a:z, :],
                                                  f32(c_hi[0:dst, a:z, :]), ALU.subtract)
                ins.then_inc(c_split, 1)

            def ternarise(half):
                w, t = weight_half(half)
                pool.wait_ge(tern_minus, half + 1)
                nc.gpsimd.tensor_tensor(t, t, w, ALU.add).then_inc(tern_sum, 1)
                pool.wait_ge(tern_sum, half + 1)
                nc.gpsimd.tensor_tensor(t, w, t, ALU.subtract).then_inc(tern, 1)

            def batch(b):
                at = Batch(b)
                if not at.first:
                    split_context(b)
                pool.wait_ge(e_free, Batch(0).use("bvo") + 1)
                pool.wait_ge(xr_loaded, 16 * b + 16)
                for t in range(TT):
                    ins = nc.gpsimd.tensor_tensor(xr[:, t, :], xr[:, t, :], tb1[:], ALU.add)
                ins.then_inc(xb_ready, 1)
                if at.first:
                    for half in range(4):
                        ternarise(half)
                pool.wait_ge(xn2_ready, b + 1)
                for t in range(TT):
                    ins = nc.gpsimd.tensor_tensor(xr[:, t, :], xr[:, t, :], tb2[:], ALU.add)
                ins.then_inc(x1b_ready, 1)

            split_context(0)
            batch(0)
            with pool.Fori(1, BATCH - 1) as b:
                batch(b)
            batch(BATCH - 1)

        @block.tensor
        def _(pe):
            def begin(count, name, bank):
                if isinstance(count, int) and count < EB:
                    return e_ps[bank]
                pe.wait_ge(e_free, count + (1 - EB))
                return e_ps[bank]

            def turn(out_, in_, n):
                return nc.tensor.transpose(out_, in_, ident[0:n, 0:n])

            def split_product(ps, parts, start, stop):
                for i, (l, r) in enumerate(parts):
                    ins = nc.tensor.matmul(ps, l, r, start=start and i == 0,
                                           stop=stop and i == len(parts) - 1)
                return ins

            def scores(b, n):
                t, c = divmod(n, NCH)
                if not (isinstance(b, int) and b == 0 and n < SB):
                    pe.wait_ge(s_masked, b * NS + (n - SB + 1))
                if t == 0:
                    g = min((CEND[c] - 1) // 512, 3)
                    if isinstance(b, int) and b == 0:
                        pe.wait_ge(e_free, PRO.index(f"C{2 * g + 1}") + 1)
                        pe.wait_ge(const_ready, 5)
                    else:
                        pe.wait_ge(e_free, Batch(b - 1).use(f"C{2 * g + 1}") + 1)
                parts = []
                for d in range(DC):
                    q = slice(t * P, (t + 1) * P)
                    k = slice(CSTART[c], CEND[c])
                    parts += [(qT_hi[:, d, q], cT_hi[:, d, k]), (qT_lo[:, d, q], cT_hi[:, d, k]),
                              (qT_hi[:, d, q], cT_lo[:, d, k])]
                split_product(s_ps[c][:, 0:CEND[c] - CSTART[c]], parts, True, True
                              ).then_inc(s_full, 1)

            def exchange(count, name, bank, b):
                kind, i = name[0], int(name[1:]) if name[1:].isdigit() else 0
                ps = begin(count, name, bank)
                if kind == "T":
                    t, c = divmod(i, 4)
                    pe.wait_ge(exp_done, 2 * TT * b + (2 * t + c // 2 + 1))
                    for j, k in enumerate(range(4 * c, min(4 * c + 4, KT))):
                        n = min(P, KEYS - k * P)
                        ins = turn(ps[0:n, j * P:(j + 1) * P],
                                   probs[:, t % 2, k * P:k * P + n], P)
                elif kind in "XY":
                    if kind == "X":
                        pe.wait_ge(xn_ready, b + 1)
                        src = xl
                    else:
                        pe.wait_ge(xn2_ready, b + 1)
                        src = xn2
                    for t in range(TT):
                        ins = turn(ps[:, t * P:(t + 1) * P], src[:, t, i * P:(i + 1) * P], P)
                elif kind == "C":
                    g, d = divmod(i, DC)
                    pe.wait_ge(raw_loaded, 32 * b + 32)
                    for j, k in enumerate(range(4 * g, min(4 * g + 4, KT))):
                        n = min(P, KEYS - k * P)
                        ins = turn(ps[:, j * P:j * P + n], raw[0:n, k, d * P:(d + 1) * P], n)
                elif kind == "Q":
                    pe.wait_ge(e_free, count + (1 - EB))
                    parts = []
                    for d in range(DC):
                        m = slice(i * P, (i + 1) * P)
                        parts += [(m_hi[:, d, m], xT_hi[:, d, :]), (m_hi[:, d, m], xT_lo[:, d, :]),
                                  (m_lo[:, d, m], xT_hi[:, d, :])]
                    ins = split_product(ps[:], parts, True, True)
                elif kind == "O":
                    pe.wait_ge(attn_split, b + 1)
                    for j in range(2):
                        q = slice((2 * i + j) * P, (2 * i + j + 1) * P)
                        parts = []
                        for d in range(DC):
                            parts += [(pt_hi[:, FT + d, q], vo_hi[:, d, :]),
                                      (pt_lo[:, FT + d, q], vo_hi[:, d, :]),
                                      (pt_hi[:, FT + d, q], vo_lo[:, d, :])]
                        ins = split_product(ps[:, j * D:(j + 1) * D], parts, True, True)
                elif kind == "H":
                    parts = []
                    for d in range(DC):
                        w = w1T[:, d, i * P:(i + 1) * P]
                        parts += [(w, xT_hi[:, d, :]), (w, xT_lo[:, d, :])]
                    ins = split_product(ps[:], parts, True, True)
                elif name in ("WqT", "WkT", "WvT"):
                    w = ("WqT", "WkT", "WvT").index(name)
                    pe.wait_ge(vo_loaded if w == 2 else qk_loaded, 32)
                    for e in range(DC):
                        for r in range(DC):
                            ins = turn(ps[:, e * D + r * P:e * D + (r + 1) * P],
                                       wraw[:, w, r, e * P:(e + 1) * P], P)
                elif name in ("M", "Wvo"):
                    pe.wait_ge(e_free, count)
                    w = 0 if name == "M" else 2
                    for r in range(DC):
                        for e in range(DC):
                            right = wT[:, 1, e, :] if name == "M" else wraw[:, 3, e, :]
                            ins = nc.tensor.matmul(ps[:, r * D:(r + 1) * D],
                                                   wT[:, w, e, r * P:(r + 1) * P], right,
                                                   start=e == 0, stop=e == DC - 1)
                elif name == "UC":
                    pe.wait_ge(rep_ready, 1)
                    for col, w, left, right in (
                            (0, D, lambda e: rep[:, 0, e, :], lambda e: wT[:, 0, e, :]),
                            (D, 1, lambda e: rep[:, 0, e, :], lambda e: bqc[:, e:e + 1]),
                            (D + 1, 1, lambda e: wT[:, 1, e, 0:P], lambda e: bqc[:, e:e + 1]),
                            (D + 2, 1, lambda e: wT[:, 1, e, P:D], lambda e: bqc[:, e:e + 1])):
                        for e in range(DC):
                            ins = nc.tensor.matmul(ps[:, col:col + w], left(e), right(e),
                                                   start=e == 0, stop=e == DC - 1)
                elif name == "bvo":
                    pe.wait_ge(rep_ready, 2)
                    for e in range(DC):
                        ins = nc.tensor.matmul(ps[:, 0:D], rep[:, 1, e, :], wraw[:, 3, e, :],
                                               start=e == 0, stop=e == DC - 1)
                elif kind == "S":
                    pe.wait_ge(wsum_ready, i)
                    ins = nc.tensor.matmul(ps[:, 0:1], ones[:], wsum[:], start=True, stop=True)
                elif kind == "A":
                    pe.wait_ge(tern, i // 2 + 1)
                    for f in range(4):
                        ins = turn(ps[:, f * P:(f + 1) * P],
                                   tmp[:, f * D + (i % 2) * P:f * D + (i % 2 + 1) * P], P)
                elif kind == "B":
                    pe.wait_ge(tern, 2 + i // 2 + 1)
                    for f in range(2):
                        for d in range(DC):
                            at = d * 512 + (2 * (i % 2) + f) * P
                            ins = turn(ps[:, f * D + d * P:f * D + (d + 1) * P],
                                       tmp[:, at:at + P], P)
                ins.then_inc(e_full, 1)

            def prologue():
                pe.wait_ge(const_ready, 5)
                for i, name in enumerate(PRO):
                    exchange(i, name, i % EB, 0)
                for n in range(AHEAD):
                    scores(0, n)

            def one(at, name):
                b = at.b + 1 if name[0] in "XQC" else at.b
                exchange(at.use(name), name, at.bank(name), b)

            def batch(b):
                at = Batch(b)
                for n in range(AHEAD, NS):
                    scores(b, n)
                    for name in at.plan["score"][n]:
                        one(at, name)
                for name in at.plan["drain"]:
                    one(at, name)
                pe.wait_ge(c_split, b + 1)
                if not at.first:
                    pe.wait_ge(y_taken, b * TT)
                for k in range(KT):
                    if k % 4 == 0:
                        pe.wait_ge(e_free, at.use(f"T{12 + k // 4}") + 1)
                    n = min(P, KEYS - k * P)
                    for d in range(DC):
                        w = slice(d * P, (d + 1) * P)
                        ins = split_product(acc[d][:], [(c_hi[0:n, k, w], pt_hi[0:n, k, :]),
                                                        (c_hi[0:n, k, w], pt_lo[0:n, k, :]),
                                                        (c_lo[0:n, k, w], pt_hi[0:n, k, :])],
                                            k == 0, k == KT - 1)
                    if k == KT - 1:
                        ins.then_inc(pv_full, 1)
                    for name in at.plan["key"][k]:
                        one(at, name)
                if not at.last:
                    scores(b + 1, 0)
                    scores(b + 1, 1)
                one(at, "O0")
                one(at, "O1")
                if not at.last:
                    for n in range(2, AHEAD):
                        scores(b + 1, n)
                one(at, "Y0")
                one(at, "Y1")
                pe.wait_ge(e_free, at.use("Y1") + 1)
                one(at, "H0")
                one(at, "H1")
                for f in range(FT):
                    pe.wait_ge(e_free, at.use(f"H{f}") + 1)
                    for t in range(TT):
                        q = slice(t * P, (t + 1) * P)
                        ps = acc[t // 2][:, (t % 2) * D:(t % 2 + 1) * D]
                        for i, h in enumerate((pt_hi, pt_lo)):
                            ins = nc.tensor.matmul(ps, h[:, f, q], w2T[:, f, :],
                                                   start=f == 0 and t % 2 == 0 and i == 0,
                                                   stop=f == FT - 1 and t % 2 == 1 and i == 1,
                                                   skip_group_check=True)
                        if f == FT - 1 and t % 2 == 1:
                            ins.then_inc(y_full, 1)
                    if f + 2 < FT:
                        one(at, f"H{f + 2}")

            prologue()
            batch(0)
            with pe.Fori(1, BATCH - 1) as b:
                batch(b)
            batch(BATCH - 1)

        def shape_of(name):
            kind, i = name[0], int(name[1:]) if name[1:].isdigit() else 0
            if kind == "T":
                t, c = divmod(i, 4)
                n = min(4, KT - 4 * c)
                rows = P if c < 3 else KREM
                return ((pt_hi, pt_lo), rows,
                        lambda a: a[0:rows, 4 * c:4 * c + n, t * P:(t + 1) * P], n * P, n)
            if kind in "XY":
                return (xT_hi, xT_lo), P, lambda a: a[:, i, :], TOK, 1
            if kind == "Q":
                return (qT_hi, qT_lo), P, lambda a: a[:, i, :], TOK, 1
            if kind == "C":
                g, d = divmod(i, DC)
                w = min(512, KEYS - 512 * g)
                return (cT_hi, cT_lo), P, lambda a: a[:, d, 512 * g:512 * g + w], w, 1
            if name == "M":
                return (m_hi, m_lo), P, lambda a: a[:], DC * D, DC
            if name == "Wvo":
                return (vo_hi, vo_lo), P, lambda a: a[:], DC * D, DC

        def psum_view(bank, rows, width, parts):
            v = e_ps[bank][0:rows, 0:width]
            return v.rearrange("p (a n) -> p a n", a=parts) if parts > 1 else v

        @block.scalar
        def _(act):
            def high(count, name, bank, b):
                (dst, _), rows, pick, width, parts = shape_of(name)
                act.wait_ge(e_full, count + 1)
                bias, scale = 0.0, 1.0
                if name[0] == "Q":
                    i = int(name[1])
                    bias = uc[:, 1 + i:2 + i]
                if name == "M":
                    scale = SCALE
                nc.scalar.activation(pick(dst), psum_view(bank, rows, width, parts),
                                     ACT.Identity, bias=bias, scale=scale).then_inc(e_hi, 1)

            def one(at, name):
                if not by_act(name):
                    return
                b = at.b + 1 if name[0] in "XQC" else at.b
                high(at.use(name), name, at.bank(name), b)

            def add_r(b, n):
                t, c = divmod(n, NCH)
                if n == 0:
                    act.wait_ge(r_ready, b + 1)
                act.wait_ge(s_full, b * NS + (n + 1))
                w = CEND[c] - CSTART[c]
                nc.scalar.activation(s_ps[c][:, 0:w], s_ps[c][:, 0:w], ACT.Identity,
                                     bias=r_now[:, t:t + 1]).then_inc(s_biased, 1)

            def exps(b, t, h):
                if h == 0:
                    act.wait_ge(max_ready, b * TT + (t + 1))
                v = probs[:, t % 2, 0:HALF] if h == 0 else probs[:, t % 2, HALF:KEYS]
                nc.scalar.activation(v, v, ACT.Exp, bias=nmax[:, t:t + 1],
                                     accum_out=sums[:, t, h:h + 1]).then_inc(exp_done, 1)

            act.wait_ge(bias_loaded, 8 * 16)
            nc.scalar.activation(tg[:], graw[:], ACT.Tanh).then_inc(gate_ready, 1)
            for i, name in enumerate(PRO):
                if name == "Q0":
                    act.wait_ge(e_free, PRO.index("UC") + 1)
                if by_act(name):
                    high(i, name, i % EB, 0)

            def head(b):
                add_r(b, 0)
                add_r(b, 1)
                add_r(b, 2)
                add_r(b, 3)
                exps(b, 0, 0)
                exps(b, 0, 1)
                add_r(b, 4)
                add_r(b, 5)

            def batch(b):
                at = Batch(b)
                for n in range(AHEAD, NS):
                    add_r(b, n)
                    t, c = divmod(n, NCH)
                    if c == 0:
                        exps(b, t - 1, 1) if t > 1 else None
                    for name in at.plan["score"][n]:
                        one(at, name)
                    if c == NCH - 1 and t < TT - 1:
                        exps(b, t, 0)
                for i, name in enumerate(at.plan["drain"]):
                    one(at, name)
                    if i < 2:
                        exps(b, TT - 1, i)
                for k in range(KT):
                    for name in at.plan["key"][k]:
                        one(at, name)
                act.wait_ge(pv_full, b + 1)
                for d in range(DC):
                    nc.scalar.activation(pt_hi[:, FT + d, :], acc[d][:],
                                         ACT.Identity).then_inc(attn_hi, 1)
                if not at.last:
                    head(b + 1)
                one(at, "Y0")
                one(at, "Y1")
                for f in range(FT):
                    name = f"H{f}"
                    act.wait_ge(e_full, at.use(name) + 1)
                    if f > 1:
                        act.wait_ge(e_free, at.use(f"H{f - 2}") + 1)
                    nc.scalar.activation(hid[:, f % 2, :], e_ps[at.bank(name)][:], ACT.Gelu,
                                         bias=b1c[:, f:f + 1]).then_inc(e_hi, 1)

            head(0)
            batch(0)
            with act.Fori(1, BATCH - 1) as b:
                batch(b)
            batch(BATCH - 1)

        @block.vector
        def _(dve):
            step = {"base": 0, "n": 0}

            def link(ins):
                step["n"] += 1
                ins.then_inc(dve_step, 1)
                dve.wait_ge(dve_step, step["base"] + step["n"])

            def pin(i):
                nc.vector.memset(gate[:, i:i + 1], 0.0)

            def low(count, hi_count, name, bank, b):
                (dhi, dlo), rows, pick, width, parts = shape_of(name)
                dve.wait_ge(e_hi, hi_count + 1)
                ps, hi = psum_view(bank, rows, width, parts), f32(pick(dhi))
                if name[0] == "Q" or name == "M":
                    i = int(name[1]) if name[0] == "Q" else 0
                    ins = nc.vector.scalar_tensor_tensor(
                        out=pick(dlo), in0=ps, in1=hi, op1=ALU.subtract,
                        scalar=uc[:, 1 + i:2 + i] if name[0] == "Q" else SCALE,
                        op0=ALU.add if name[0] == "Q" else ALU.mult)
                else:
                    ins = nc.vector.tensor_tensor(pick(dlo), ps, hi, ALU.subtract)
                ins.then_inc(e_free, 1)

            def take(count, name, bank):
                kind, i = name[0], int(name[1:]) if name[1:].isdigit() else 0
                dve.wait_ge(e_full, count + 1)
                ps = e_ps[bank]
                if name in ("WqT", "WkT", "WvT"):
                    w = ("WqT", "WkT", "WvT").index(name)
                    ins = nc.vector.tensor_copy(
                        wT[:, w, :, :], ps[:].rearrange("p (e r) -> p e r", e=DC))
                elif name == "UC":
                    nc.vector.tensor_copy(U[:], ps[:, 0:D])
                    ins = nc.vector.tensor_scalar(uc[:], ps[:, D:D + 3], SCALE, None, ALU.mult)
                elif name == "bvo":
                    link(nc.vector.tensor_tensor(tb1[:], ps[:, 0:D], tb1[:], ALU.add))
                    nc.vector.tensor_scalar(tb1[:], tb1[:], tg[:, 0:1], None, ALU.mult)
                    ins = nc.vector.tensor_scalar(tb2[:], tb2[:], tg[:, 1:2], None, ALU.mult)
                elif kind == "S":
                    link(nc.vector.tensor_scalar(wsum[:], ps[:, 0:1], 1.0 / (FF * D), 1e-8,
                                                 ALU.mult, ALU.max))
                    nc.vector.tensor_scalar(thr[:, 0:1], wsum[:], 0.5, None, ALU.mult)
                    ins = nc.vector.tensor_scalar(thr[:, 1:2], wsum[:], -0.5, None, ALU.mult)
                elif kind == "A":
                    ins = nc.vector.tensor_copy(w1T[:, i % 2, (i // 2) * 512:(i // 2 + 1) * 512],
                                                ps[:])
                elif kind == "B":
                    ins = nc.vector.tensor_copy(w2T[:, 2 * i:2 * i + 2, :],
                                                ps[:].rearrange("p (f d) -> p f d", f=2))
                ins.then_inc(e_free, 1)

            def one(at, name):
                if by_act(name):
                    b = at.b + 1 if name[0] in "XQC" else at.b
                    low(at.use(name), at.hi(name), name, at.bank(name), b)
                else:
                    take(at.use(name), name, at.bank(name))

            def mask_scores(b, n):
                t, c = divmod(n, NCH)
                dve.wait_ge(s_biased, b * NS + (n + 1))
                pin(n)
                w = min(CEND[c], KEYS) - CSTART[c]
                k = slice(CSTART[c], CSTART[c] + w)
                nc.vector.tensor_tensor_reduce(probs[:, t % 2, k], s_ps[c][:, 0:w], mbias[:, t, k],
                                               1.0, MASKED, ALU.add, ALU.max,
                                               cmax[:, c:c + 1]).then_inc(s_masked, 1)
                if c == NCH - 1:
                    dve.wait_ge(s_masked, b * NS + (n + 1))
                    nc.vector.tensor_reduce(nmax[:, t:t + 1], cmax[:], AX.X, ALU.max,
                                            negate=True).then_inc(max_ready, 1)

            def ln_stats(src):
                for t in range(TT):
                    ins = nc.vector.bn_stats(stats[:, t, :], src[:, t, :])
                link(ins)
                pin(NS if src is xl else NS + 1)
                for t in range(TT):
                    ins = nc.vector.bn_aggr(mv[:, t, :], stats[:, t, :])
                link(ins)

            def ln_seed():
                link(nc.vector.tensor_scalar(var[:], mv[:, :, 1], EPS, None, ALU.add))
                nc.vector.tensor_scalar(nhalf[:], var[:], -0.5, None, ALU.mult)
                link(nc.vector.tensor_scalar(rt[:].bitcast(I32), var[:].bitcast(I32), 1, None,
                                             ALU.logical_shift_right))
                link(nc.vector.tensor_scalar(rs[:].bitcast(I32), rt[:].bitcast(I32), -1.0,
                                             float(RSQRT_SEED), ALU.mult, ALU.add))

            def ln_newton():
                link(nc.vector.tensor_tensor(rt[:], rs[:], rs[:], ALU.mult))
                link(nc.vector.tensor_tensor(rt[:], rt[:], nhalf[:], ALU.mult))
                link(nc.vector.scalar_tensor_tensor(out=rs[:], in0=rt[:], scalar=1.5, in1=rs[:],
                                                    op0=ALU.add, op1=ALU.mult))

            def ln_apply(src, dst, done):
                for t in range(TT):
                    ins = nc.vector.tensor_scalar(dst[:, t, :], src[:, t, :], mv[:, t, 0:1],
                                                  rs[:, t:t + 1], ALU.subtract, ALU.mult)
                ins.then_inc(done, 1)

            def row_terms(b):
                dve.wait_ge(xn_ready, b + 1)
                pin(NS + 4)
                for t in range(TT):
                    ins = nc.vector.tensor_tensor_reduce(junk[:, t % 2, :], xl[:, t, :], U[:],
                                                         SCALE, uc[:, 0:1], ALU.mult, ALU.add,
                                                         r_next[:, t:t + 1])
                    if t % 2:
                        link(ins)
                        pin(NS + 2 + t // 2)

            def publish_r():
                nc.vector.tensor_copy(r_now[:], r_next[:]).then_inc(r_ready, 1)

            def rows_gain(b):
                dve.wait_ge(exp_done, 2 * TT * b + 2 * TT)
                link(nc.vector.tensor_tensor(tot[:], sums[:, :, 0], sums[:, :, 1], ALU.add))
                link(nc.vector.reciprocal(rec[:], tot[:]))
                link(nc.vector.tensor_scalar(gain[:], rec[:], tg[:, 0:1], None, ALU.mult))

            def attended(at, i):
                name = f"O{i}"
                if i == 0:
                    dve.wait_ge(xb_ready, at.b + 1)
                dve.wait_ge(e_full, at.use(name) + 1)
                for j in range(2):
                    t = 2 * i + j
                    ins = nc.vector.scalar_tensor_tensor(
                        out=xr[:, t, :], in0=e_ps[at.bank(name)][:, j * D:(j + 1) * D],
                        scalar=gain[:, t:t + 1], in1=xr[:, t, :], op0=ALU.mult, op1=ALU.add)
                ins.then_inc(e_free, 1)

            def mask_to_bias(t):
                dve.wait_ge(mask_loaded[t], 16)
                nc.vector.tensor_scalar(mbias[:, t, :], mask_i[:, t, :], 0, MASKED, ALU.is_equal,
                                        ALU.mult).then_inc(mask_ready, 1)

            dve.wait_ge(xl_loaded, 16)
            ln_stats(xl)
            ln_seed()
            for _ in range(3):
                ln_newton()
            ln_apply(xl, xl, xn_ready)
            dve.wait_ge(bias_loaded, 8 * 16)
            dve.wait_ge(const_ready, 5)
            dve.wait_ge(gate_ready, 1)
            for e in range(DC):
                ins = nc.vector.tensor_scalar(rep[:, 0, e, :], ones[:], bkc[:, e:e + 1], None,
                                              ALU.mult)
            ins.then_inc(rep_ready, 1)
            for e in range(DC):
                ins = nc.vector.tensor_scalar(rep[:, 1, e, :], ones[:], bvc[:, e:e + 1], None,
                                              ALU.mult)
            ins.then_inc(rep_ready, 1)
            for i, name in enumerate(PRO):
                if by_act(name):
                    low(i, pro_hi(name), name, i % EB, 0)
                else:
                    take(i, name, i % EB)
                if name == "UC":
                    dve.wait_ge(e_free, i + 1)
                    row_terms(0)
                    publish_r()
            mask_to_bias(0)

            def head_a(b):
                mask_scores(b, 0)
                mask_scores(b, 1)

            mask_to_bias_at = {AHEAD: 2, AHEAD + 2: 3}
            dve.wait_ge(mask_ready, 1)
            head_a(0)
            mask_scores(0, 2)
            mask_scores(0, 3)
            mask_to_bias(1)
            dve.wait_ge(mask_ready, 2)
            mask_scores(0, 4)
            mask_scores(0, 5)
            pro_steps = step["n"]

            def batch(b, base):
                at = Batch(b)
                step["base"], step["n"] = base, 0
                for n in range(AHEAD, NS):
                    if at.first and n in mask_to_bias_at:
                        mask_to_bias(mask_to_bias_at[n])
                        dve.wait_ge(mask_ready, mask_to_bias_at[n] + 1)
                    mask_scores(b, n)
                    for name in at.plan["score"][n]:
                        one(at, name)
                        if at.first and name == "S1":
                            half_ternary(0)
                        if at.first and name == "A1":
                            half_ternary(1)
                    if at.first and n == AHEAD + 1:
                        sum_of_weights(1)
                    if not at.last:
                        if n == AHEAD + 3:
                            dve.wait_ge(xl_loaded, 16 * b + 32)
                            ln_stats(xl)
                        elif n == AHEAD + 4:
                            ln_seed()
                        elif n == AHEAD + 5:
                            ln_newton()
                        elif n == AHEAD + 6:
                            ln_newton()
                            ln_newton()
                        elif n == AHEAD + 7:
                            ln_apply(xl, xl, xn_ready)
                        elif n == AHEAD + 8:
                            row_terms(b + 1)
                for name in at.plan["drain"]:
                    if name == "Q1":
                        publish_r()
                    one(at, name)
                for k in range(KT):
                    for name in at.plan["key"][k]:
                        one(at, name)
                        if at.first and name == "S2":
                            half_ternary(2)
                        if at.first and name == "B1":
                            half_ternary(3)
                    if k == 1:
                        rows_gain(b)
                    if at.first and k == 5:
                        sum_of_weights(2)
                for d in range(DC):
                    dve.wait_ge(attn_hi, b * DC + (d + 1))
                    ins = nc.vector.tensor_tensor(pt_lo[:, FT + d, :], acc[d][:],
                                                  f32(pt_hi[:, FT + d, :]), ALU.subtract)
                ins.then_inc(attn_split, 1)
                if not at.last:
                    head_a(b + 1)
                attended(at, 0)
                attended(at, 1)
                dve.wait_ge(e_free, at.use("O1") + 1)
                ln_stats(xr)
                if not at.last:
                    mask_scores(b + 1, 2)
                ln_seed()
                if not at.last:
                    mask_scores(b + 1, 3)
                ln_newton()
                ln_newton()
                if not at.last:
                    mask_scores(b + 1, 4)
                ln_newton()
                ln_apply(xr, xn2, xn2_ready)
                if not at.last:
                    mask_scores(b + 1, 5)
                one(at, "Y0")
                one(at, "Y1")
                for f in range(FT):
                    dve.wait_ge(e_hi, at.hi(f"H{f}") + 1)
                    nc.vector.tensor_copy(pt_hi[:, f, :], hid[:, f % 2, :]).then_inc(h_hi, 1)
                    dve.wait_ge(h_hi, b * FT + (f + 1))
                    nc.vector.tensor_tensor(pt_lo[:, f, :], hid[:, f % 2, :],
                                            f32(pt_hi[:, f, :]), ALU.subtract).then_inc(e_free, 1)
                for t in range(TT):
                    if t == 0:
                        dve.wait_ge(x1b_ready, b + 1)
                    if t % 2 == 0:
                        dve.wait_ge(y_full, b * 2 + (t // 2 + 1))
                    nc.vector.scalar_tensor_tensor(
                        out=xr[:, t, :], in0=acc[t // 2][:, (t % 2) * D:(t % 2 + 1) * D],
                        scalar=tg[:, 1:2], in1=xr[:, t, :], op0=ALU.mult,
                        op1=ALU.add).then_inc(y_taken, 1)
                return step["n"]

            def sum_of_weights(i):
                src = w1raw if i == 1 else w2raw
                dve.wait_ge(w1_loaded if i == 1 else w2_loaded, 16)
                nc.vector.tensor_reduce(wsum[:], src[:], AX.XY, ALU.add,
                                        apply_absolute_value=True).then_inc(wsum_ready, 1)

            def half_ternary(h):
                w, t = weight_half(h)
                dve.wait_ge(e_free, Batch(0).use(("S1", "A1", "S2", "B1")[h]) + 1)
                link(nc.vector.tensor_scalar(t, w, thr[:, 0:1], None, ALU.is_gt))
                nc.vector.scalar_tensor_tensor(out=t, in0=w, scalar=thr[:, 1:2], in1=t,
                                               op0=ALU.is_lt, op1=ALU.subtract
                                               ).then_inc(tern_minus, 1)

            n0 = batch(0, pro_steps)
            with dve.Fori(1, BATCH - 1) as b:
                n1 = batch(b, (b - 1) * BODY_STEPS + (pro_steps + n0))
            assert n1 == BODY_STEPS, n1
            batch(BATCH - 1, (BATCH - 2) * BODY_STEPS + pro_steps + n0)


_INS = ['x', 'ctx_1024', 'mask_SxS2_ik0', 'g_xattn', 'g_ffn', 'L0_xattn_Wq', 'L0_xattn_bq',
        'L0_xattn_Wk', 'L0_xattn_bk', 'L0_xattn_Wv', 'L0_xattn_bv', 'L0_xattn_Wo', 'L0_xattn_bo',
        'L0_ffn_W1', 'L0_ffn_b1', 'L0_ffn_W2', 'L0_ffn_b2']


def kernel(**inputs):
    import numpy as _np
    import concourse.bacc as _bacc
    from concourse import mybir as _mybir
    from concourse.bass_utils import run_bass_kernel_spmd as _run

    nc = _bacc.Bacc("TRN2", target_bir_lowering=False, num_devices=1)
    arrays, args = {}, []
    for name in _INS:
        a = _np.ascontiguousarray(inputs[name])
        arrays[f"in_{name}_dram"] = a
        args.append(nc.dram_tensor(f"in_{name}_dram", a.shape, _mybir.dt.from_np(a.dtype),
                                   kind="ExternalInput").ap())
    args.append(nc.dram_tensor("out_dram", (BATCH, TOK, D), _mybir.dt.float32,
                               kind="ExternalOutput").ap())
    build(nc, *args)
    r = _run(nc, [arrays], core_ids=[0])
    return r.results[0]["out_dram"]
```

```python
from contextlib import ExitStack

import concourse.bass as bass
from concourse import mybir

F32 = mybir.dt.float32
F32R = mybir.dt.float32r
BF16 = mybir.dt.bfloat16
I32 = mybir.dt.int32
ALU = mybir.AluOpType
ACT = mybir.ActivationFunctionType
AX = mybir.AxisListType

P = 128
BATCH, TOK, D = 4, 512, 256
KEYS = 1601
FF = 1024
TT = TOK // P
DC = D // P
KT = -(-KEYS // P)
KREM = KEYS - (KT - 1) * P
KEYS2 = KEYS + KEYS % 2
FT = FF // P
NCH = 4
CW = -(-KEYS2 // NCH)
CW += CW % 2
CSTART = [0] + [KEYS2 - (NCH - 1 - c) * (CW - 2) - (CW - 2) for c in range(1, NCH)]
CEND = CSTART[1:] + [KEYS2]
NS = TT * NCH
AHEAD = 2 * NCH
HALF = 2 * 4 * P
EPS = 1e-5
SCALE = 0.25
MASKED = -float(2.0 ** 127)
RSQRT_SEED = 0x5F3759DF
EB = 4
SB = 2

PRO = ["WqT", "WkT", "M", "UC", "X0", "X1", "C0", "C1", "Q0", "Q1"] + [f"C{i}" for i in range(2, 8)]
PRO_SCORES = {"C3": [0], "C5": [1], "C7": [2, 3, 4, 5, 6, 7]}
SCORE = {n: [f"T{n - AHEAD}"] for n in range(AHEAD, NS)}
KEY = [{0: ["T8"], 1: ["T9"], 2: ["T10"], 3: ["T11"], 4: ["T12"], 5: ["T13"], 6: ["T14"],
        7: ["T15"], 8: ["C0"], 9: ["X0"], 10: ["X1"], 11: ["C1"], 12: ["Q0"]},
       {0: ["Q1"], 1: ["C2"], 2: ["O0", "C3"], 3: ["C4"], 4: ["C5"], 5: ["C6"], 6: ["C7"],
        7: ["N0"], 8: ["N1"], 9: ["N2"], 11: ["N3"], 12: ["Y0"]}]
TAIL = ["H0", "O1", "H1", "N4", "H2", "F0", "N5", "H3", "F1", "N6", "Y1", "F2", "N7", "H4",
        "F3", "H5", "H6", "F4", "H7", "F5", "F6", "F7"]
FIRST_SCORE = {8: ["S1", "WvT"], 9: ["Wvo"], 10: ["bvo"], 13: ["A0", "A1"]}
FIRST_KEY = [{1: ["A2", "A3"], 9: ["S2"]},
             {3: ["B0", "B1"], 6: ["B2", "B3", "O0"]}]


def uses(first, last):
    def keep(names):
        return [u for u in names if not (last and u[0] in "XQCN") and not (first and u == "O0")]
    plan = {"score": {n: SCORE[n] + (FIRST_SCORE.get(n, []) if first else []) for n in SCORE}}
    plan["key"] = [{k: keep(KEY[h].get(k, [])) + (FIRST_KEY[h].get(k, []) if first else [])
                    for k in range(KT)} for h in range(2)]
    plan["tail"] = [u for u in TAIL if not (last and u[0] == "N")]
    order = sum(plan["score"].values(), [])
    for h in range(2):
        order += sum(plan["key"][h].values(), [])
    order += plan["tail"]
    return plan, [u for u in order if u[0] not in "NF"]


FIRST_PLAN, FIRST = uses(True, False)
MID_PLAN, MID = uses(False, False)
LAST_PLAN, LAST = uses(False, True)
ALONE = ("O", "W", "U", "b", "S", "A", "B")


def by_act(name):
    return name == "Wvo" or name[0] not in ALONE


class Batch:

    def __init__(self, b):
        self.b = b
        self.first = isinstance(b, int) and b == 0
        self.last = isinstance(b, int) and b == BATCH - 1
        self.plan, self.order = ((FIRST_PLAN, FIRST) if self.first else
                                 (LAST_PLAN, LAST) if self.last else (MID_PLAN, MID))

    def base(self, order_len, first_len, pro_len):
        if self.first:
            return pro_len
        return (self.b - 1) * order_len + (pro_len + first_len)

    def use(self, name):
        return self.base(len(MID), len(FIRST), len(PRO)) + self.order.index(name)

    def bank(self, name):
        at = 0 if self.first else len(FIRST)
        return (len(PRO) + at + self.order.index(name)) % EB

    def hi(self, name):
        n = [sum(map(by_act, o)) for o in (MID, FIRST, PRO)]
        return self.base(*n) + sum(map(by_act, self.order[:self.order.index(name)]))


assert len(MID) % EB == 0 and NS % SB == 0


def pro_hi(name):
    return sum(map(by_act, PRO[:PRO.index(name)]))


LN_STEPS = 2 + 3 + 3 * 3
ROW_STEPS = 2
GAIN_STEPS = 3
BODY_STEPS = 3 * LN_STEPS + ROW_STEPS + GAIN_STEPS


def build(nc, x, ctx_in, mask, g_x, g_f, Wq, bq, Wk, bk, Wv, bv, Wo, bo, W1, b1, W2, b2, out):
    with ExitStack() as stack:
        def sb(name, shape, dt):
            return stack.enter_context(nc.sbuf_tensor(name, shape, dt))

        def sem(name):
            return stack.enter_context(nc.semaphore(name))

        place = [(nc.sbuf_base + 31) // 32 * 32]

        def region(name, shape, dt):
            n = 1
            for s in shape[1:]:
                n *= s
            at = place[0]
            place[0] += (n * (2 if dt == BF16 else 4) + 31) // 32 * 32
            return nc.alloc_sbuf_tensor_at(name, shape, dt, offset=at), at

        def alias(name, shape, dt, at):
            return nc.alloc_sbuf_tensor_at(name, shape, dt, offset=at)

        pt_hi, _ = region("pt_hi", [P, KT, TOK], F32R)
        pt_lo, _ = region("pt_lo", [P, KT, TOK], F32R)
        c_hi, c_at = region("c_hi", [P, KT, D], F32R)
        c_lo, _ = region("c_lo", [P, KT, D], F32R)
        cT_hi, _ = region("cT_hi", [P, DC, KEYS2], F32R)
        cT_lo, _ = region("cT_lo", [P, DC, KEYS2], F32R)
        raw, _ = region("raw", [P, KT, D], F32)
        probs, _ = region("probs", [P, 2, KEYS], F32)
        mbias, _ = region("mbias", [P, TT, KEYS], BF16)
        qT_hi, _ = region("qT_hi", [P, DC, TOK], F32R)
        qT_lo, _ = region("qT_lo", [P, DC, TOK], F32R)
        xT_hi, _ = region("xT_hi", [P, DC, TOK], F32R)
        xT_lo, _ = region("xT_lo", [P, DC, TOK], F32R)
        xl, _ = region("xl", [P, TT, D], F32)
        xr, _ = region("xr", [P, TT, D], F32)
        hid, tmp_at = region("hid", [P, 4, TOK], F32)
        xn2, _ = region("xn2", [P, TT, D], F32)
        w1T, w1T_at = region("w1T", [P, DC, FF], F32R)
        w2T, w2T_at = region("w2T", [P, FT, D], F32R)
        m_hi, _ = region("m_hi", [P, DC, D], F32R)
        m_lo, _ = region("m_lo", [P, DC, D], F32R)
        vo_hi, _ = region("vo_hi", [P, DC, D], F32R)
        vo_lo, _ = region("vo_lo", [P, DC, D], F32R)
        junk, _ = region("junk", [P, 2, D], BF16)
        U, _ = region("U", [P, D], F32)
        tb1, _ = region("tb1", [P, D], F32)
        tb2, _ = region("tb2", [P, D], F32)
        ident, _ = region("ident", [P, P], F32)
        bqc, _ = region("bqc", [P, DC], F32)
        bkc, _ = region("bkc", [P, DC], F32)
        bvc, _ = region("bvc", [P, DC], F32)
        b1c, _ = region("b1c", [P, FT], F32)
        uc, _ = region("uc", [P, 3], F32)
        tg, _ = region("tg", [P, 2], F32)
        graw, _ = region("graw", [P, 2], F32)
        cmax, _ = region("cmax", [P, 2, NCH], F32)
        nmax, _ = region("nmax", [P, TT], F32)
        sums, _ = region("sums", [P, TT, 2], F32)
        tot, _ = region("tot", [P, TT], F32)
        rec, _ = region("rec", [P, TT], F32)
        gain, _ = region("gain", [P, TT], F32)
        r_next, _ = region("r_next", [P, TT], F32)
        r_now, _ = region("r_now", [P, TT], F32)
        stats, _ = region("stats", [P, TT, 6], F32)
        mv, _ = region("mv", [P, TT, 2], F32)
        var, _ = region("var", [P, TT], F32)
        nhalf, _ = region("nhalf", [P, TT], F32)
        rs, _ = region("rs", [P, TT], F32)
        rt, _ = region("rt", [P, TT], F32)
        wsum, _ = region("wsum", [P, 1], F32)
        thr, _ = region("thr", [P, 2], F32)
        gate, _ = region("gate", [P, NS + 6], F32)
        pgate, _ = region("pgate", [P, 2], F32)
        ones, ones_at = region("ones", [P, P], F32)
        assert place[0] <= nc.sbuf_usable_end, place[0]
        mask_i = alias("mask_i", [P, TT, KEYS], I32, c_at)
        wraw = alias("wraw", [P, 4, DC, D], F32, w2T_at)
        wT = alias("wT", [P, 3, DC, D], F32, w1T_at)
        rep = alias("rep", [P, 2, DC, P], F32, w1T_at + 3 * DC * D * 4)
        tmp = alias("tmp", [P, 2 * TOK], F32, tmp_at)
        hid_at = tmp_at + 2 * TOK * 4
        w1raw = alias("w1raw", [P, FT, D], F32, hid_at)
        w2raw = alias("w2raw", [P, DC, FF], F32, hid_at)

        s_ps = [stack.enter_context(nc.psum_tensor(f"s_ps{i}", [P, 512], F32)) for i in range(SB)]
        e_ps = [stack.enter_context(nc.psum_tensor(f"e_ps{i}", [P, 512], F32)) for i in range(EB)]
        acc = [stack.enter_context(nc.psum_tensor(f"acc{i}", [P, 512], F32)) for i in range(2)]

        e_full, e_hi, e_free = sem("e_full"), sem("e_hi"), sem("e_free")
        s_full, s_biased, s_masked = sem("s_full"), sem("s_biased"), sem("s_masked")
        max_ready, exp_done = sem("max_ready"), sem("exp_done")
        pv_full, attn_hi, attn_split = sem("pv_full"), sem("attn_hi"), sem("attn_split")
        y_full, y_taken = sem("y_full"), sem("y_taken")
        xn_ready, xn2_ready, r_ready = sem("xn_ready"), sem("xn2_ready"), sem("r_ready")
        xl_loaded, xr_loaded, raw_loaded = sem("xl_loaded"), sem("xr_loaded"), sem("raw_loaded")
        xb_ready, x1b_ready = sem("xb_ready"), sem("x1b_ready")
        c_split, pool_step, dve_step = sem("c_split"), sem("pool_step"), sem("dve_step")
        qk_loaded, vo_loaded, bias_loaded = sem("qk_loaded"), sem("vo_loaded"), sem("bias_loaded")
        qk_bias_loaded = sem("qk_bias_loaded")
        mask_loaded = [sem(f"mask_loaded{t}") for t in range(TT)]
        mask_ready = sem("mask_ready")
        w1_loaded, w2_loaded, gate_ready = sem("w1_loaded"), sem("w2_loaded"), sem("gate_ready")
        const_ready, ident_zero = sem("const_ready"), sem("ident_zero")
        tern_minus, tern_sum, tern = sem("tern_minus"), sem("tern_sum"), sem("tern")
        h_hi, c_hi_ready = sem("h_hi"), sem("c_hi_ready")
        wsum_ready, rep_ready = sem("wsum_ready"), sem("rep_ready")
        out_stored = sem("out_stored")

        xv = x.rearrange("b (t p) d -> b p t d", p=P)
        ov = out.rearrange("b (t p) d -> b p t d", p=P)
        cfull = ctx_in[:, 0:(KT - 1) * P, :].rearrange("b (t p) d -> b p t d", p=P)
        crem = ctx_in[:, (KT - 1) * P:KEYS, :]

        def of(ap, b, pat):
            return ap[bass.ds(b, 1)].rearrange(pat)

        def f32(ap):
            return ap.bitcast(F32)

        def weight_half(h):
            if h < 2:
                return w1raw[:, 4 * h:4 * h + 4, :], tmp[:].rearrange("p (f d) -> p f d", d=D)
            return (w2raw[:, :, (h - 2) * 512:(h - 1) * 512],
                    tmp[:].rearrange("p (c f) -> p c f", c=DC))

        block = stack.enter_context(nc.Block())

        @block.sync
        def _(sp):
            def load_x(dst, b, done):
                sp.dma_start(dst[:], of(xv, b, "b p t d -> (b p) t d")).then_inc(done, 16)

            def load_context(b):
                sp.dma_start(raw[:, 0:KT - 1, :],
                             of(cfull, b, "b p t d -> (b p) t d")).then_inc(raw_loaded, 16)
                sp.dma_start(raw[0:KREM, KT - 1, :],
                             of(crem, b, "b p d -> (b p) d")).then_inc(raw_loaded, 16)

            def load_weight(i, w, done):
                sp.dma_start(wraw[:, i, :, :], w.rearrange("(c p) n -> p c n", p=P)
                             ).then_inc(done, 16)

            def load_column(dst, src, done):
                sp.dma_start(dst[:], src.rearrange("(c p) -> p c", p=P),
                             allow_slow_non_contiguous=True).then_inc(done, 16)

            load_weight(0, Wq, qk_loaded)
            load_weight(1, Wk, qk_loaded)
            load_x(xl, 0, xl_loaded)
            load_column(bkc, bk, qk_bias_loaded)
            load_column(bqc, bq, qk_bias_loaded)
            load_context(0)
            for t in range(TT):
                sp.dma_start(mask_i[:, t, :], mask[t * P:(t + 1) * P, :]
                             ).then_inc(mask_loaded[t], 16)
                if t == 1:
                    for i, g in enumerate((g_x, g_f)):
                        sp.dma_start(graw[:, i:i + 1], g.partition_broadcast(P)
                                     ).then_inc(bias_loaded, 16)
                    load_column(bvc, bv, bias_loaded)
                    load_weight(2, Wv, vo_loaded)
                    load_weight(3, Wo, vo_loaded)
                    for dst, src in ((tb1, bo), (tb2, b2)):
                        sp.dma_start(dst[:], src.partition_broadcast(P)).then_inc(bias_loaded, 16)
                    load_column(b1c, b1, bias_loaded)
                if t == 2:
                    sp.dma_start(w1raw[:], W1.rearrange("(t p) d -> p t d", p=P)
                                 ).then_inc(w1_loaded, 16)

            def batch(b):
                at = Batch(b)
                if not at.last:
                    if at.first:
                        sp.wait_ge(r_ready, 1)
                    else:
                        sp.wait_ge(e_full, at.base(len(MID), len(FIRST), len(PRO)))
                    load_x(xl, b + 1, xl_loaded)
                if not at.first:
                    sp.wait_ge(out_stored, b * (16 * 2))
                load_x(xr, b, xr_loaded)
                if at.first:
                    sp.wait_ge(e_full, at.use("A3") + 1)
                    sp.dma_start(w2raw[:], W2.rearrange("(c p) f -> p c f", p=P)
                                 ).then_inc(w2_loaded, 16)
                if not at.last:
                    sp.wait_ge(c_split, b + 1)
                    if at.first:
                        sp.wait_ge(e_full, len(PRO))
                    load_context(b + 1)
                for h in range(2):
                    sp.wait_ge(y_taken, b * TT + 2 * h + 2)
                    sp.dma_start(of(ov, b, "b p t d -> (b p) t d")[:, 2 * h:2 * h + 2, :],
                                 xr[:, 2 * h:2 * h + 2, :]).then_inc(out_stored, 16)

            batch(0)
            with sp.Fori(1, BATCH - 1) as b:
                batch(b)
            batch(BATCH - 1)
            sp.wait_ge(out_stored, BATCH * 2 * 16)

        @block.gpsimd
        def _(pool):
            nc.gpsimd.memset(ident[:], 0.0).then_inc(ident_zero, 1)
            nc.gpsimd.memset(ones[:], 1.0).then_inc(const_ready, 1)
            nc.gpsimd.memset(pgate[:], 0.0).then_inc(const_ready, 1)
            nc.gpsimd.memset(f32(cT_hi[:, :, KEYS:KEYS2]), 0.0).then_inc(const_ready, 1)
            nc.gpsimd.memset(f32(cT_lo[:, :, KEYS:KEYS2]), 0.0).then_inc(const_ready, 1)
            pool.wait_ge(ident_zero, 1)
            nc.gpsimd.affine_select(out=ident[:], in_=ident[:], compare_op=ALU.not_equal, fill=1.0,
                                    base=0, pattern=[[-1, P]],
                                    channel_multiplier=1).then_inc(const_ready, 1)
            pool.wait_ge(const_ready, 5)

            def split_context(b):
                pool.wait_ge(c_hi_ready, b + 1)
                for dst, a, z in ((P, 0, KT - 1), (KREM, KT - 1, KT)):
                    ins = nc.gpsimd.tensor_tensor(c_lo[0:dst, a:z, :], raw[0:dst, a:z, :],
                                                  f32(c_hi[0:dst, a:z, :]), ALU.subtract)
                ins.then_inc(c_split, 1)

            def ternarise(half):
                w, t = weight_half(half)
                pool.wait_ge(tern_minus, half + 1)
                nc.gpsimd.tensor_tensor(t, t, w, ALU.add).then_inc(tern_sum, 1)
                pool.wait_ge(tern_sum, half + 1)
                nc.gpsimd.tensor_tensor(w, w, t, ALU.subtract).then_inc(tern, 1)

            def batch(b):
                at = Batch(b)
                if not at.first:
                    split_context(b)
                pool.wait_ge(e_free, Batch(0).use("bvo") + 1)
                pool.wait_ge(xr_loaded, 16 * b + 16)
                for t in range(TT):
                    ins = nc.gpsimd.tensor_tensor(xr[:, t, :], xr[:, t, :], tb1[:], ALU.add)
                ins.then_inc(xb_ready, 1)
                if at.first:
                    ternarise(2)
                    ternarise(3)
                for h in range(2):
                    pool.wait_ge(xn2_ready, 2 * b + (h + 1))
                    for t in range(2 * h, 2 * h + 2):
                        ins = nc.gpsimd.tensor_tensor(xr[:, t, :], xr[:, t, :], tb2[:], ALU.add)
                    ins.then_inc(x1b_ready, 1)

            ternarise(0)
            ternarise(1)
            split_context(0)
            batch(0)
            with pool.Fori(1, BATCH - 1) as b:
                batch(b)
            batch(BATCH - 1)

        @block.tensor
        def _(pe):
            def begin(count, name, bank):
                if isinstance(count, int) and count < EB:
                    return e_ps[bank]
                pe.wait_ge(e_free, count + (1 - EB))
                return e_ps[bank]

            def turn(out_, in_, n):
                return nc.tensor.transpose(out_, in_, ident[0:n, 0:n])

            def split_product(ps, parts, start, stop):
                for i, (l, r) in enumerate(parts):
                    ins = nc.tensor.matmul(ps, l, r, start=start and i == 0,
                                           stop=stop and i == len(parts) - 1)
                return ins

            def scores(b, n):
                t, c = divmod(n, NCH)
                if not (isinstance(b, int) and b == 0 and n < SB):
                    pe.wait_ge(s_masked, b * NS + (n - SB + 1))
                if t == 0:
                    g = min((CEND[c] - 1) // 512, 3)
                    if isinstance(b, int) and b == 0:
                        pe.wait_ge(e_free, max(PRO.index(f"C{2 * g + 1}"), PRO.index("Q1")) + 1)
                        pe.wait_ge(const_ready, 5)
                    else:
                        pe.wait_ge(e_free, Batch(b - 1).use(f"C{2 * g + 1}") + 1)
                parts = []
                for d in range(DC):
                    q = slice(t * P, (t + 1) * P)
                    k = slice(CSTART[c], CEND[c])
                    parts += [(qT_hi[:, d, q], cT_hi[:, d, k]), (qT_lo[:, d, q], cT_hi[:, d, k]),
                              (qT_hi[:, d, q], cT_lo[:, d, k])]
                split_product(s_ps[c % SB][:, 0:CEND[c] - CSTART[c]], parts, True, True
                              ).then_inc(s_full, 1)

            def exchange(count, name, bank, b):
                kind, i = name[0], int(name[1:]) if name[1:].isdigit() else 0
                ps = begin(count, name, bank)
                if kind == "T":
                    t, c = divmod(i, 4)
                    pe.wait_ge(exp_done, 2 * TT * b + (2 * t + c // 2 + 1))
                    for j, k in enumerate(range(4 * c, min(4 * c + 4, KT))):
                        n = min(P, KEYS - k * P)
                        ins = turn(ps[0:n, j * P:(j + 1) * P],
                                   probs[:, t % 2, k * P:k * P + n], P)
                elif kind == "X":
                    pe.wait_ge(xn_ready, b + 1)
                    for t in range(TT):
                        ins = turn(ps[:, t * P:(t + 1) * P], xl[:, t, i * P:(i + 1) * P], P)
                elif kind == "Y":
                    pe.wait_ge(xn2_ready, 2 * b + (i + 1))
                    for d in range(DC):
                        for j in range(2):
                            ins = turn(ps[:, (2 * d + j) * P:(2 * d + j + 1) * P],
                                       xn2[:, 2 * i + j, d * P:(d + 1) * P], P)
                elif kind == "C":
                    g, d = divmod(i, DC)
                    pe.wait_ge(raw_loaded, 32 * b + 32)
                    for j, k in enumerate(range(4 * g, min(4 * g + 4, KT))):
                        n = min(P, KEYS - k * P)
                        ins = turn(ps[:, j * P:j * P + n], raw[0:n, k, d * P:(d + 1) * P], n)
                elif kind == "Q":
                    if isinstance(b, int) and b == 0:
                        pe.wait_ge(e_free, PRO.index("X1") + 1)
                    else:
                        pe.wait_ge(e_free, Batch(b - 1).use("X1") + 1)
                    parts = []
                    for d in range(DC):
                        m = slice(i * P, (i + 1) * P)
                        parts += [(m_hi[:, d, m], xT_hi[:, d, :]), (m_hi[:, d, m], xT_lo[:, d, :]),
                                  (m_lo[:, d, m], xT_hi[:, d, :])]
                    ins = split_product(ps[:], parts, True, True)
                elif kind == "O":
                    pe.wait_ge(attn_split, 2 * b + (i + 1))
                    for j in range(2):
                        q = slice((2 * i + j) * P, (2 * i + j + 1) * P)
                        parts = []
                        for d in range(DC):
                            parts += [(pt_hi[:, FT + d, q], vo_hi[:, d, :]),
                                      (pt_lo[:, FT + d, q], vo_hi[:, d, :]),
                                      (pt_hi[:, FT + d, q], vo_lo[:, d, :])]
                        ins = split_product(ps[:, j * D:(j + 1) * D], parts, True, True)
                elif kind == "H":
                    h, g = divmod(i, 4)
                    if g == 0:
                        pe.wait_ge(e_free, Batch(b).use(f"Y{h}") + 1)
                    q = slice(2 * h * P, 2 * (h + 1) * P)
                    for j in range(2):
                        parts = []
                        for d in range(DC):
                            w = w1T[:, d, (2 * g + j) * P:(2 * g + j + 1) * P]
                            parts += [(w, xT_hi[:, d, q]), (w, xT_lo[:, d, q])]
                        ins = split_product(ps[:, j * D:(j + 1) * D], parts, True, True)
                elif name in ("WqT", "WkT", "WvT"):
                    w = ("WqT", "WkT", "WvT").index(name)
                    pe.wait_ge(vo_loaded if w == 2 else qk_loaded, 32)
                    for e in range(DC):
                        for r in range(DC):
                            ins = turn(ps[:, e * D + r * P:e * D + (r + 1) * P],
                                       wraw[:, w, r, e * P:(e + 1) * P], P)
                elif name in ("M", "Wvo"):
                    pe.wait_ge(e_free, count)
                    w = 0 if name == "M" else 2
                    for r in range(DC):
                        for e in range(DC):
                            right = wT[:, 1, e, :] if name == "M" else wraw[:, 3, e, :]
                            ins = nc.tensor.matmul(ps[:, r * D:(r + 1) * D],
                                                   wT[:, w, e, r * P:(r + 1) * P], right,
                                                   start=e == 0, stop=e == DC - 1)
                elif name == "UC":
                    pe.wait_ge(rep_ready, 1)
                    for col, w, left, right in (
                            (0, D, lambda e: rep[:, 0, e, :], lambda e: wT[:, 0, e, :]),
                            (D, 1, lambda e: rep[:, 0, e, :], lambda e: bqc[:, e:e + 1]),
                            (D + 1, 1, lambda e: wT[:, 1, e, 0:P], lambda e: bqc[:, e:e + 1]),
                            (D + 2, 1, lambda e: wT[:, 1, e, P:D], lambda e: bqc[:, e:e + 1])):
                        for e in range(DC):
                            ins = nc.tensor.matmul(ps[:, col:col + w], left(e), right(e),
                                                   start=e == 0, stop=e == DC - 1)
                elif name == "bvo":
                    pe.wait_ge(rep_ready, 2)
                    for e in range(DC):
                        ins = nc.tensor.matmul(ps[:, 0:D], rep[:, 1, e, :], wraw[:, 3, e, :],
                                               start=e == 0, stop=e == DC - 1)
                elif kind == "S":
                    pe.wait_ge(wsum_ready, i)
                    ins = nc.tensor.matmul(ps[:, 0:1], ones[:], wsum[:], start=True, stop=True)
                elif kind == "A":
                    pe.wait_ge(tern, i // 2 + 1)
                    for f in range(4):
                        ins = turn(ps[:, f * P:(f + 1) * P],
                                   w1raw[:, 4 * (i // 2) + f, (i % 2) * P:(i % 2 + 1) * P], P)
                elif kind == "B":
                    pe.wait_ge(tern, 2 + i // 2 + 1)
                    for f in range(2):
                        for d in range(DC):
                            at = (2 * i + f) * P
                            ins = turn(ps[:, f * D + d * P:f * D + (d + 1) * P],
                                       w2raw[:, d, at:at + P], P)
                ins.then_inc(e_full, 1)

            def prologue():
                pe.wait_ge(const_ready, 5)
                for i, name in enumerate(PRO):
                    exchange(i, name, i % EB, 0)
                    for n in PRO_SCORES.get(name, []):
                        scores(0, n)

            def one(at, name):
                b = at.b + 1 if name[0] in "XQC" else at.b
                exchange(at.use(name), name, at.bank(name), b)

            def attend(at, h):
                if not at.first:
                    pe.wait_ge(y_taken, (at.b - 1) * TT + (2 * h + 2))
                q = slice(2 * h * P, 2 * (h + 1) * P)
                for k in range(KT):
                    if k % 4 == 0:
                        pe.wait_ge(e_free, at.use(f"T{8 * h + 4 + k // 4}") + 1)
                    n = min(P, KEYS - k * P)
                    for d in range(DC):
                        w = slice(d * P, (d + 1) * P)
                        parts = [(c_hi[0:n, k, w], pt_hi[0:n, k, q]),
                                 (c_hi[0:n, k, w], pt_lo[0:n, k, q]),
                                 (c_lo[0:n, k, w], pt_hi[0:n, k, q])]
                        for i, (l, r) in enumerate(parts):
                            ins = nc.tensor.matmul(acc[h][:, d * D:(d + 1) * D], l, r,
                                                   start=k == 0 and d == 0 and i == 0,
                                                   stop=k == KT - 1 and d == DC - 1 and i == 2,
                                                   skip_group_check=True)
                    if k == KT - 1:
                        ins.then_inc(pv_full, 1)
                    for name in at.plan["key"][h][k]:
                        step(at, name)

            def step(at, name):
                if name[0] == "N":
                    scores(at.b + 1, int(name[1:]))
                elif name[0] == "F":
                    second_product(at, int(name[1:]))
                else:
                    one(at, name)

            def second_product(at, i):
                h, g = divmod(i, 4)
                pe.wait_ge(e_free, at.use(f"H{i}") + 1)
                for f in (2 * g, 2 * g + 1):
                    for t in (2 * h, 2 * h + 1):
                        q = slice(t * P, (t + 1) * P)
                        for j, part in enumerate((pt_hi, pt_lo)):
                            ins = nc.tensor.matmul(acc[h][:, (t % 2) * D:(t % 2 + 1) * D],
                                                   part[:, f, q], w2T[:, f, :],
                                                   start=f == 0 and t % 2 == 0 and j == 0,
                                                   stop=f == FT - 1 and t % 2 == 1 and j == 1,
                                                   skip_group_check=True)
                if g == 3:
                    ins.then_inc(y_full, 1)

            def batch(b):
                at = Batch(b)
                for n in range(AHEAD, NS):
                    for name in at.plan["score"][n]:
                        one(at, name)
                    scores(b, n)
                pe.wait_ge(c_split, b + 1)
                attend(at, 0)
                attend(at, 1)
                for name in at.plan["tail"]:
                    step(at, name)

            prologue()
            batch(0)
            with pe.Fori(1, BATCH - 1) as b:
                batch(b)
            batch(BATCH - 1)

        def shape_of(name):
            kind, i = name[0], int(name[1:]) if name[1:].isdigit() else 0
            if kind == "T":
                t, c = divmod(i, 4)
                n = min(4, KT - 4 * c)
                rows = P if c < 3 else KREM
                return ((pt_hi, pt_lo), rows,
                        lambda a: a[0:rows, 4 * c:4 * c + n, t * P:(t + 1) * P], n * P, n)
            if kind == "X":
                return (xT_hi, xT_lo), P, lambda a: a[:, i, :], TOK, 1
            if kind == "Y":
                return ((xT_hi, xT_lo), P, lambda a: a[:, :, 2 * i * P:2 * (i + 1) * P],
                        TOK, DC)
            if kind == "Q":
                return (qT_hi, qT_lo), P, lambda a: a[:, i, :], TOK, 1
            if kind == "C":
                g, d = divmod(i, DC)
                w = min(512, KEYS - 512 * g)
                return (cT_hi, cT_lo), P, lambda a: a[:, d, 512 * g:512 * g + w], w, 1
            if name == "M":
                return (m_hi, m_lo), P, lambda a: a[:], DC * D, DC
            if name == "Wvo":
                return (vo_hi, vo_lo), P, lambda a: a[:], DC * D, DC

        def psum_view(bank, rows, width, parts):
            v = e_ps[bank][0:rows, 0:width]
            return v.rearrange("p (a n) -> p a n", a=parts) if parts > 1 else v

        @block.scalar
        def _(act):
            def high(count, name, bank, b):
                (dst, _), rows, pick, width, parts = shape_of(name)
                act.wait_ge(e_full, count + 1)
                bias, scale = 0.0, 1.0
                if name[0] == "Q":
                    i = int(name[1])
                    bias = uc[:, 1 + i:2 + i]
                if name == "M":
                    scale = SCALE
                nc.scalar.activation(pick(dst), psum_view(bank, rows, width, parts),
                                     ACT.Identity, bias=bias, scale=scale).then_inc(e_hi, 1)

            def one(at, name):
                if not by_act(name):
                    return
                b = at.b + 1 if name[0] in "XQC" else at.b
                high(at.use(name), name, at.bank(name), b)

            def add_r(b, n):
                t, c = divmod(n, NCH)
                if n == 0:
                    act.wait_ge(r_ready, b + 1)
                act.wait_ge(s_full, b * NS + (n + 1))
                w = CEND[c] - CSTART[c]
                nc.scalar.activation(s_ps[c % SB][:, 0:w], s_ps[c % SB][:, 0:w], ACT.Identity,
                                     bias=r_now[:, t:t + 1]).then_inc(s_biased, 1)

            def exps(b, t, h):
                if h == 0:
                    act.wait_ge(max_ready, b * TT + (t + 1))
                v = probs[:, t % 2, 0:HALF] if h == 0 else probs[:, t % 2, HALF:KEYS]
                nc.scalar.activation(v, v, ACT.Exp, bias=nmax[:, t:t + 1],
                                     accum_out=sums[:, t, h:h + 1]).then_inc(exp_done, 1)

            def context_high(b, piece):
                if piece == 0:
                    act.wait_ge(raw_loaded, 32 * b + 32)
                    if isinstance(b, int) and b == 0:
                        act.wait_ge(mask_ready, TT)
                k = slice(4 * piece, min(4 * piece + 4, KT))
                n = P if piece < 3 else KREM
                ins = nc.scalar.activation(c_hi[0:n, k, :], raw[0:n, k, :], ACT.Identity)
                if piece == 3:
                    ins.then_inc(c_hi_ready, 1)

            def attention_high(b, h):
                act.wait_ge(pv_full, 2 * b + (h + 1))
                nc.scalar.activation(pt_hi[:, FT:FT + DC, 2 * h * P:2 * (h + 1) * P],
                                     acc[h][:].rearrange("p (d q) -> p d q", d=DC),
                                     ACT.Identity).then_inc(attn_hi, 1)

            def hidden(at, i):
                name = f"H{i}"
                act.wait_ge(e_full, at.use(name) + 1)
                if i >= 4:
                    act.wait_ge(e_free, at.use(f"H{i - 4}") + 1)
                for j in range(2):
                    f = 2 * (i % 4) + j
                    ins = nc.scalar.activation(hid[:, i % 4, j * D:(j + 1) * D],
                                               e_ps[at.bank(name)][:, j * D:(j + 1) * D],
                                               ACT.Gelu, bias=b1c[:, f:f + 1])
                ins.then_inc(e_hi, 1)

            def batch(b):
                at = Batch(b)
                exps(b, 1, 0)
                exps(b, 1, 1)
                for n in range(AHEAD, NS):
                    for name in at.plan["score"][n]:
                        one(at, name)
                    if at.first and 9 <= n < 13:
                        context_high(0, n - 9)
                    add_r(b, n)
                    if n == AHEAD + NCH:
                        exps(b, 2, 0)
                    if n == AHEAD + NCH + 1:
                        exps(b, 2, 1)
                for h in range(2):
                    for k in range(KT):
                        if h == 0 and k in (1, 3):
                            exps(b, 3, k // 2)
                        for name in at.plan["key"][h][k]:
                            step(at, name)
                        if h == 1 and k == 0:
                            attention_high(b, 0)
                if not at.last:
                    exps(b + 1, 0, 0)
                    exps(b + 1, 0, 1)
                attention_high(b, 1)
                for name in at.plan["tail"]:
                    step(at, name)
                    if name in ("H0", "H1", "H2", "H3") and not at.last:
                        context_high(b + 1, int(name[1:]))

            def step(at, name):
                if name[0] == "N":
                    add_r(at.b + 1, int(name[1:]))
                elif name[0] == "H":
                    hidden(at, int(name[1:]))
                elif name[0] != "F":
                    one(at, name)

            for i, name in enumerate(PRO):
                if name == "Q0":
                    act.wait_ge(e_free, PRO.index("UC") + 1)
                if by_act(name):
                    high(i, name, i % EB, 0)
                for n in PRO_SCORES.get(name, []):
                    add_r(0, n)
                    if n == NCH:
                        exps(0, 0, 0)
                        exps(0, 0, 1)
            act.wait_ge(bias_loaded, 6 * 16)
            nc.scalar.activation(tg[:], graw[:], ACT.Tanh).then_inc(gate_ready, 1)
            batch(0)
            with act.Fori(1, BATCH - 1) as b:
                batch(b)
            batch(BATCH - 1)

        @block.vector
        def _(dve):
            step = {"base": 0, "n": 0}

            def link(ins):
                step["n"] += 1
                ins.then_inc(dve_step, 1)
                dve.wait_ge(dve_step, step["base"] + step["n"])

            def pin(i):
                nc.vector.memset(gate[:, i:i + 1], 0.0)

            def low(count, hi_count, name, bank, b):
                (dhi, dlo), rows, pick, width, parts = shape_of(name)
                dve.wait_ge(e_hi, hi_count + 1)
                ps, hi = psum_view(bank, rows, width, parts), f32(pick(dhi))
                if name[0] == "Q" or name == "M":
                    i = int(name[1]) if name[0] == "Q" else 0
                    ins = nc.vector.scalar_tensor_tensor(
                        out=pick(dlo), in0=ps, in1=hi, op1=ALU.subtract,
                        scalar=uc[:, 1 + i:2 + i] if name[0] == "Q" else SCALE,
                        op0=ALU.add if name[0] == "Q" else ALU.mult)
                else:
                    ins = nc.vector.tensor_tensor(pick(dlo), ps, hi, ALU.subtract)
                ins.then_inc(e_free, 1)

            def take(count, name, bank):
                kind, i = name[0], int(name[1:]) if name[1:].isdigit() else 0
                dve.wait_ge(e_full, count + 1)
                ps = e_ps[bank]
                if name in ("WqT", "WkT", "WvT"):
                    w = ("WqT", "WkT", "WvT").index(name)
                    ins = nc.vector.tensor_copy(
                        wT[:, w, :, :], ps[:].rearrange("p (e r) -> p e r", e=DC))
                elif name == "UC":
                    nc.vector.tensor_copy(U[:], ps[:, 0:D])
                    ins = nc.vector.tensor_scalar(uc[:], ps[:, D:D + 3], SCALE, None, ALU.mult)
                elif name == "bvo":
                    link(nc.vector.tensor_tensor(tb1[:], ps[:, 0:D], tb1[:], ALU.add))
                    nc.vector.tensor_scalar(tb1[:], tb1[:], tg[:, 0:1], None, ALU.mult)
                    ins = nc.vector.tensor_scalar(tb2[:], tb2[:], tg[:, 1:2], None, ALU.mult)
                elif kind == "S":
                    link(nc.vector.tensor_scalar(wsum[:], ps[:, 0:1], 1.0 / (FF * D), 1e-8,
                                                 ALU.mult, ALU.max))
                    nc.vector.tensor_scalar(thr[:, 0:1], wsum[:], 0.5, None, ALU.mult)
                    ins = nc.vector.tensor_scalar(thr[:, 1:2], wsum[:], -0.5, None, ALU.mult)
                elif kind == "A":
                    ins = nc.vector.tensor_copy(w1T[:, i % 2, (i // 2) * 512:(i // 2 + 1) * 512],
                                                ps[:])
                elif kind == "B":
                    ins = nc.vector.tensor_copy(w2T[:, 2 * i:2 * i + 2, :],
                                                ps[:].rearrange("p (f d) -> p f d", f=2))
                ins.then_inc(e_free, 1)

            def one(at, name):
                if by_act(name):
                    b = at.b + 1 if name[0] in "XQC" else at.b
                    low(at.use(name), at.hi(name), name, at.bank(name), b)
                else:
                    take(at.use(name), name, at.bank(name))

            def mask_scores(b, n):
                t, c = divmod(n, NCH)
                dve.wait_ge(s_biased, b * NS + (n + 1))
                pin(n)
                w = min(CEND[c], KEYS) - CSTART[c]
                k = slice(CSTART[c], CSTART[c] + w)
                nc.vector.tensor_tensor_reduce(probs[:, t % 2, k], s_ps[c % SB][:, 0:w], mbias[:, t, k],
                                               1.0, MASKED, ALU.add, ALU.max,
                                               cmax[:, t % 2, c:c + 1]).then_inc(s_masked, 1)
                if c == NCH - 1:
                    dve.wait_ge(s_masked, b * NS + (n + 1))
                    nc.vector.tensor_reduce(nmax[:, t:t + 1], cmax[:, t % 2, :], AX.X, ALU.max,
                                            negate=True).then_inc(max_ready, 1)

            def ln_stats(src, first=0, end=TT):
                for t in range(first, end):
                    ins = nc.vector.bn_stats(stats[:, t, :], src[:, t, :])
                link(ins)
                pin(NS if src is xl else NS + 1 + first // 2)
                for t in range(first, end):
                    ins = nc.vector.bn_aggr(mv[:, t, :], stats[:, t, :])
                link(ins)

            def ln_seed():
                link(nc.vector.tensor_scalar(var[:], mv[:, :, 1], EPS, None, ALU.add))
                nc.vector.tensor_scalar(nhalf[:], var[:], -0.5, None, ALU.mult)
                link(nc.vector.tensor_scalar(rt[:].bitcast(I32), var[:].bitcast(I32), 1, None,
                                             ALU.logical_shift_right))
                link(nc.vector.tensor_scalar(rs[:].bitcast(I32), rt[:].bitcast(I32), -1.0,
                                             float(RSQRT_SEED), ALU.mult, ALU.add))

            def ln_newton():
                link(nc.vector.tensor_tensor(rt[:], rs[:], rs[:], ALU.mult))
                link(nc.vector.tensor_tensor(rt[:], rt[:], nhalf[:], ALU.mult))
                link(nc.vector.scalar_tensor_tensor(out=rs[:], in0=rt[:], scalar=1.5, in1=rs[:],
                                                    op0=ALU.add, op1=ALU.mult))

            def ln_apply(src, dst, done, first=0, end=TT):
                for t in range(first, end):
                    ins = nc.vector.tensor_scalar(dst[:, t, :], src[:, t, :], mv[:, t, 0:1],
                                                  rs[:, t:t + 1], ALU.subtract, ALU.mult)
                ins.then_inc(done, 1)

            def row_terms(b):
                dve.wait_ge(xn_ready, b + 1)
                pin(NS + 5)
                for t in range(TT):
                    ins = nc.vector.tensor_tensor_reduce(junk[:, t % 2, :], xl[:, t, :], U[:],
                                                         SCALE, uc[:, 0:1], ALU.mult, ALU.add,
                                                         r_next[:, t:t + 1])
                    if t % 2:
                        link(ins)
                        pin(NS + 3 + t // 2)

            def publish_r():
                nc.vector.tensor_copy(r_now[:], r_next[:]).then_inc(r_ready, 1)

            def rows_gain(b):
                dve.wait_ge(exp_done, 2 * TT * b + 2 * TT)
                link(nc.vector.tensor_tensor(tot[:], sums[:, :, 0], sums[:, :, 1], ALU.add))
                link(nc.vector.reciprocal(rec[:], tot[:]))
                link(nc.vector.tensor_scalar(gain[:], rec[:], tg[:, 0:1], None, ALU.mult))

            def attended(at, i):
                name = f"O{i}"
                if i == 0:
                    dve.wait_ge(xb_ready, at.b + 1)
                dve.wait_ge(e_full, at.use(name) + 1)
                for j in range(2):
                    t = 2 * i + j
                    ins = nc.vector.scalar_tensor_tensor(
                        out=xr[:, t, :], in0=e_ps[at.bank(name)][:, j * D:(j + 1) * D],
                        scalar=gain[:, t:t + 1], in1=xr[:, t, :], op0=ALU.mult, op1=ALU.add)
                ins.then_inc(e_free, 1)

            def mask_to_bias(t):
                dve.wait_ge(mask_loaded[t], 16)
                nc.vector.tensor_scalar(mbias[:, t, :], mask_i[:, t, :], 0, MASKED, ALU.is_equal,
                                        ALU.mult).then_inc(mask_ready, 1)

            def sum_of_weights(i):
                src = w1raw if i == 1 else w2raw
                dve.wait_ge(w1_loaded if i == 1 else w2_loaded, 16)
                nc.vector.tensor_reduce(wsum[:], src[:], AX.XY, ALU.add,
                                        apply_absolute_value=True).then_inc(wsum_ready, 1)

            def half_ternary(h):
                w, t = weight_half(h)
                if h % 2 == 0:
                    dve.wait_ge(e_free, Batch(0).use(("S1", "S2")[h // 2]) + 1)
                if h > 0:
                    dve.wait_ge(tern, h)
                link(nc.vector.tensor_scalar(t, w, thr[:, 0:1], None, ALU.is_gt))
                nc.vector.scalar_tensor_tensor(out=t, in0=w, scalar=thr[:, 1:2], in1=t,
                                               op0=ALU.is_lt, op1=ALU.subtract
                                               ).then_inc(tern_minus, 1)

            def replicate(i, column):
                for e in range(DC):
                    ins = nc.vector.tensor_scalar(rep[:, i, e, :], ones[:], column[:, e:e + 1],
                                                  None, ALU.mult)
                ins.then_inc(rep_ready, 1)

            for i, name in enumerate(PRO):
                if by_act(name):
                    low(i, pro_hi(name), name, i % EB, 0)
                else:
                    take(i, name, i % EB)
                if name == "WkT":
                    dve.wait_ge(xl_loaded, 16)
                    ln_stats(xl)
                    dve.wait_ge(qk_bias_loaded, 32)
                    dve.wait_ge(const_ready, 5)
                    replicate(0, bkc)
                    ln_seed()
                    for _ in range(3):
                        ln_newton()
                    ln_apply(xl, xl, xn_ready)
                if name == "X1":
                    dve.wait_ge(e_free, PRO.index("UC") + 1)
                    row_terms(0)
                    publish_r()
                if name == "C1":
                    mask_to_bias(0)
                for n in PRO_SCORES.get(name, []):
                    if n % NCH == 0:
                        dve.wait_ge(mask_ready, n // NCH + 1)
                    mask_scores(0, n)
                    if n == 0:
                        mask_to_bias(1)
                    if n in (5, 6):
                        mask_to_bias(n - 3)
            sum_of_weights(1)
            dve.wait_ge(bias_loaded, 6 * 16)
            replicate(1, bvc)
            pro_steps = step["n"]

            def attention_low(b, h):
                q = slice(2 * h * P, 2 * (h + 1) * P)
                dve.wait_ge(attn_hi, 2 * b + (h + 1))
                nc.vector.tensor_tensor(pt_lo[:, FT:FT + DC, q],
                                        acc[h][:].rearrange("p (d q) -> p d q", d=DC),
                                        f32(pt_hi[:, FT:FT + DC, q]),
                                        ALU.subtract).then_inc(attn_split, 1)

            def hidden_parts(at, i):
                h, g = divmod(i, 4)
                src = hid[:, i % 4, :].rearrange("p (f q) -> p f q", f=2)
                dst = (slice(None), slice(2 * g, 2 * g + 2), slice(2 * h * P, 2 * (h + 1) * P))
                dve.wait_ge(e_hi, at.hi(f"H{i}") + 1)
                nc.vector.tensor_copy(pt_hi[dst], src).then_inc(h_hi, 1)
                dve.wait_ge(h_hi, at.b * 8 + (i + 1))
                nc.vector.tensor_tensor(pt_lo[dst], src, f32(pt_hi[dst]),
                                        ALU.subtract).then_inc(e_free, 1)

            def store_ready(at, h):
                dve.wait_ge(x1b_ready, 2 * at.b + (h + 1))
                dve.wait_ge(y_full, 2 * at.b + (h + 1))
                for t in (2 * h, 2 * h + 1):
                    nc.vector.scalar_tensor_tensor(
                        out=xr[:, t, :], in0=acc[h][:, (t % 2) * D:(t % 2 + 1) * D],
                        scalar=tg[:, 1:2], in1=xr[:, t, :], op0=ALU.mult,
                        op1=ALU.add).then_inc(y_taken, 1)

            def step_of(at, name):
                kind, i = name[0], int(name[1:])
                if kind == "N":
                    mask_scores(at.b + 1, i)
                elif kind == "H":
                    hidden_parts(at, i)
                elif kind == "O":
                    attended(at, i)
                elif kind != "F":
                    one(at, name)
                    if name == "Q1":
                        publish_r()
                elif i % 4 == 3:
                    store_ready(at, i // 4)

            def second_ln(at, h):
                def begin():
                    dve.wait_ge(e_free, at.use(f"O{h}") + 1)
                    ln_stats(xr, 2 * h, 2 * h + 2)

                def middle():
                    ln_seed()
                    ln_newton()

                def rest():
                    ln_newton()
                    ln_newton()
                    ln_apply(xr, xn2, xn2_ready, 2 * h, 2 * h + 2)
                return [begin, middle, rest]

            def batch(b, base):
                at = Batch(b)
                step["base"], step["n"] = base, 0
                ln = {} if at.last else {
                    11: lambda: (dve.wait_ge(xl_loaded, 16 * b + 32), ln_stats(xl)),
                    12: ln_seed, 13: ln_newton, 14: ln_newton, 15: ln_newton,
                    NS + 2: lambda: ln_apply(xl, xl, xn_ready),
                    NS + 10: lambda: row_terms(b + 1)}
                for n in range(AHEAD, NS):
                    for name in at.plan["score"][n]:
                        one(at, name)
                        if name == "S1":
                            half_ternary(0)
                    if at.first and n % NCH == 0:
                        dve.wait_ge(mask_ready, n // NCH + 1)
                    mask_scores(b, n)
                    if at.first and n == AHEAD + 2:
                        half_ternary(1)
                    if n in ln:
                        ln[n]()
                for k in range(KT):
                    for name in at.plan["key"][0][k]:
                        one(at, name)
                        if name == "S2":
                            half_ternary(2)
                    if NS + k in ln:
                        ln[NS + k]()
                    if at.first and k == 8:
                        sum_of_weights(2)
                rows_gain(b)
                pieces = second_ln(at, 0)
                pieces_at = (7, 8, 9) if at.first else (3, 5, 7)
                for k in range(KT):
                    for name in at.plan["key"][1][k]:
                        step_of(at, name)
                    if k == 0:
                        attention_low(b, 0)
                    if at.first and k == 1:
                        half_ternary(3)
                    if k in pieces_at:
                        pieces[pieces_at.index(k)]()
                attention_low(b, 1)
                pieces = second_ln(at, 1)
                pieces_at = ({"O1": (0, 1, 2)} if at.last else
                             {"O1": (0,), "H1": (1,), "N4": (2,)})
                for name in at.plan["tail"]:
                    step_of(at, name)
                    for p in pieces_at.get(name, ()):
                        pieces[p]()
                return step["n"]

            n0 = batch(0, pro_steps)
            with dve.Fori(1, BATCH - 1) as b:
                n1 = batch(b, (b - 1) * BODY_STEPS + (pro_steps + n0))
            assert n1 == BODY_STEPS, n1
            batch(BATCH - 1, (BATCH - 2) * BODY_STEPS + pro_steps + n0)


_INS = ['x', 'ctx_1024', 'mask_SxS2_ik0', 'g_xattn', 'g_ffn', 'L0_xattn_Wq', 'L0_xattn_bq',
        'L0_xattn_Wk', 'L0_xattn_bk', 'L0_xattn_Wv', 'L0_xattn_bv', 'L0_xattn_Wo', 'L0_xattn_bo',
        'L0_ffn_W1', 'L0_ffn_b1', 'L0_ffn_W2', 'L0_ffn_b2']


def kernel(**inputs):
    import numpy as _np
    import concourse.bacc as _bacc
    from concourse import mybir as _mybir
    from concourse.bass_utils import run_bass_kernel_spmd as _run

    nc = _bacc.Bacc("TRN2", target_bir_lowering=False, num_devices=1)
    arrays, args = {}, []
    for name in _INS:
        a = _np.ascontiguousarray(inputs[name])
        arrays[f"in_{name}_dram"] = a
        args.append(nc.dram_tensor(f"in_{name}_dram", a.shape, _mybir.dt.from_np(a.dtype),
                                   kind="ExternalInput").ap())
    args.append(nc.dram_tensor("out_dram", (BATCH, TOK, D), _mybir.dt.float32,
                               kind="ExternalOutput").ap())
    build(nc, *args)
    r = _run(nc, [arrays], core_ids=[0])
    return r.results[0]["out_dram"]
```

```python
from contextlib import ExitStack

import concourse.bass as bass
from concourse import mybir

F32 = mybir.dt.float32
F32R = mybir.dt.float32r
BF16 = mybir.dt.bfloat16
I32 = mybir.dt.int32
ALU = mybir.AluOpType
ACT = mybir.ActivationFunctionType
AX = mybir.AxisListType

P = 128
BATCH, TOK, D = 4, 512, 256
KEYS = 1601
FF = 1024
TT = TOK // P
DC = D // P
KT = -(-KEYS // P)
KREM = KEYS - (KT - 1) * P
KEYS2 = KEYS + KEYS % 2
FT = FF // P
NCH = 4
CW = -(-KEYS2 // NCH)
CW += CW % 2
CSTART = [0] + [KEYS2 - (NCH - 1 - c) * (CW - 2) - (CW - 2) for c in range(1, NCH)]
CEND = CSTART[1:] + [KEYS2]
NS = TT * NCH
AHEAD = 2 * NCH
HALF = 2 * 4 * P
EPS = 1e-5
SCALE = 0.25
MASKED = -float(2.0 ** 127)
RSQRT_SEED = 0x5F3759DF
NEWTON_W = -0.5 * 1.5 ** 0.5
NEWTON_C = 1.5 * 1.5 ** 0.5
HALLEY_W = -0.5 / 1.5 * 1.5 ** 0.25
HALLEY_B = 2.5 / 1.5 ** 0.75
HALLEY_C = 1.875 / 1.5 ** 0.5
EB = 4
SB = 2

PRO = ["WqT", "WkT", "M", "UC", "X0", "X1", "C0", "C1", "Q0", "C2", "Q1", "C3", "C4", "C5", "C6",
       "C7", "S1", "WvT", "Wvo", "bvo"]
PRO_SCORES = {"C5": [0], "C7": [1, 2, 3, 4], "S1": [5], "WvT": [6, 7]}
SCORE = {n: [f"T{n - AHEAD}"] for n in range(AHEAD, NS)}
KEY = [{0: ["T8"], 1: ["T11", "T10"], 2: ["T9"], 3: ["T12"], 5: ["T13", "T15"], 8: ["T14", "C0"],
        10: ["X0", "X1"], 11: ["C1"], 12: ["Q0"]},
       {1: ["C2"], 2: ["Q1", "C3", "O0"], 4: ["N0", "C4", "C5"], 5: ["N1"], 7: ["C6", "C7"], 9:
        ["N2"], 11: ["Y0"]}]
TAIL = ["N3", "O1", "H0", "N4", "H1", "H2", "N5", "H3", "F0", "N6", "F1", "Y1", "F2", "N7", "F3",
        "H4", "H5", "H6", "H7", "F4", "F5", "F6", "F7"]
LAST_TAIL = ["H0", "O1", "H1", "H2", "H3", "F0", "Y1", "F1", "F2", "F3", "H4", "H5", "H6", "H7",
             "F4", "F5", "F6", "F7"]
FIRST_SCORE = {12: ["A0"], 13: ["A1"]}
FIRST_KEY = [{1: ["A2", "A3"], 8: ["S2"]},
             {3: ["B0"], 5: ["B1", "B2", "B3", "O0"]}]

EXP_AT = {2: (13, 14), 3: (1, 4), 0: ("N3", "O1")}
ROUND_AT = ("F0", "F1", "N7", "H6")
LN_AT = (10, 11, 12, 13, 14, 15, 16, 18, 20, 26)
LN2_KEY = (4, 4, 4)
FIRST_LN2_KEY = (6, 6, 6)
LN2_TAIL = ("O1", "O1", "H1")
LAST_LN2_TAIL = ("O1", "O1", "O1")
TERN1_AT = (9, 10)
W2_SUM_AT = (6, 7)
TERN2_AT = (8, 9)
TERN3_AT = (0, 1)


def uses(first, last):
    def keep(names):
        return [u for u in names if not (last and u[0] in "XQCN") and not (first and u == "O0")]
    plan = {"score": {n: SCORE[n] + (FIRST_SCORE.get(n, []) if first else []) for n in SCORE}}
    plan["key"] = [{k: keep(KEY[h].get(k, [])) + (FIRST_KEY[h].get(k, []) if first else [])
                    for k in range(KT)} for h in range(2)]
    plan["tail"] = LAST_TAIL if last else TAIL
    order = sum(plan["score"].values(), [])
    for h in range(2):
        order += sum(plan["key"][h].values(), [])
    order += plan["tail"]
    return plan, [u for u in order if u[0] not in "NF"]


FIRST_PLAN, FIRST = uses(True, False)
MID_PLAN, MID = uses(False, False)
LAST_PLAN, LAST = uses(False, True)
ALONE = ("O", "W", "U", "b", "S", "A", "B")


def by_act(name):
    return name == "Wvo" or name[0] not in ALONE


class Batch:

    def __init__(self, b):
        self.b = b
        self.first = isinstance(b, int) and b == 0
        self.last = isinstance(b, int) and b == BATCH - 1
        self.plan, self.order = ((FIRST_PLAN, FIRST) if self.first else
                                 (LAST_PLAN, LAST) if self.last else (MID_PLAN, MID))

    def base(self, order_len, first_len, pro_len):
        if self.first:
            return pro_len
        return (self.b - 1) * order_len + (pro_len + first_len)

    def use(self, name):
        return self.base(len(MID), len(FIRST), len(PRO)) + self.order.index(name)

    def use_of_last(self, *names):
        return self.use(max(names, key=self.order.index))

    def bank(self, name):
        at = 0 if self.first else len(FIRST)
        return (len(PRO) + at + self.order.index(name)) % EB

    def hi(self, name):
        n = [sum(map(by_act, o)) for o in (MID, FIRST, PRO)]
        return self.base(*n) + sum(map(by_act, self.order[:self.order.index(name)]))


assert len(MID) % EB == 0 and NS % SB == 0


def pro_hi(name):
    return sum(map(by_act, PRO[:PRO.index(name)]))


LN_STEPS = 2 + 3 + 3 + 4
ROW_STEPS = 2
GAIN_STEPS = 3
BODY_STEPS = 3 * LN_STEPS + ROW_STEPS + GAIN_STEPS


def build(nc, x, ctx_in, mask, g_x, g_f, Wq, bq, Wk, bk, Wv, bv, Wo, bo, W1, b1, W2, b2, out):
    with ExitStack() as stack:
        def sem(name):
            return stack.enter_context(nc.semaphore(name))

        place = [(nc.sbuf_base + 31) // 32 * 32]

        def region(name, shape, dt):
            n = 1
            for s in shape[1:]:
                n *= s
            at = place[0]
            place[0] += (n * (2 if dt == BF16 else 4) + 31) // 32 * 32
            return nc.alloc_sbuf_tensor_at(name, shape, dt, offset=at), at

        def alias(name, shape, dt, at):
            return nc.alloc_sbuf_tensor_at(name, shape, dt, offset=at)

        pt_hi, pt_at = region("pt_hi", [P, KT, TOK], F32R)
        pt_lo, pt_lo_at = region("pt_lo", [P, KT, TOK], F32R)
        c_hi, _ = region("c_hi", [P, KT, D], F32R)
        c_lo, _ = region("c_lo", [P, KT, D], F32R)
        cT_hi, _ = region("cT_hi", [P, DC, KEYS2], F32R)
        cT_lo, _ = region("cT_lo", [P, DC, KEYS2], F32R)
        raw, _ = region("raw", [P, KT, D], F32)
        probs, _ = region("probs", [P, 2, KEYS], F32)
        mbias, _ = region("mbias", [P, TT, KEYS], BF16)
        qT_hi, _ = region("qT_hi", [P, DC, TOK], F32R)
        qT_lo, _ = region("qT_lo", [P, DC, TOK], F32R)
        xT_hi, _ = region("xT_hi", [P, DC, TOK], F32R)
        xT_lo, _ = region("xT_lo", [P, DC, TOK], F32R)
        xl, _ = region("xl", [P, TT, D], F32)
        xr, _ = region("xr", [P, TT, D], F32)
        hid, tmp_at = region("hid", [P, 4, TOK], F32)
        xn2, _ = region("xn2", [P, TT, D], F32)
        w1T, w1T_at = region("w1T", [P, DC, FF], F32R)
        w2T, w2T_at = region("w2T", [P, FT, D], F32R)
        m_hi, _ = region("m_hi", [P, DC, D], F32R)
        m_lo, _ = region("m_lo", [P, DC, D], F32R)
        vo_hi, _ = region("vo_hi", [P, DC, D], F32R)
        vo_lo, _ = region("vo_lo", [P, DC, D], F32R)
        junk, _ = region("junk", [P, 2, D], BF16)
        U, _ = region("U", [P, D], F32)
        tb1, _ = region("tb1", [P, D], F32)
        tb2, _ = region("tb2", [P, D], F32)
        ident, _ = region("ident", [P, P], F32)
        bqc, _ = region("bqc", [P, DC], F32)
        bkc, _ = region("bkc", [P, DC], F32)
        bvc, _ = region("bvc", [P, DC], F32)
        b1c, _ = region("b1c", [P, FT], F32)
        uc, _ = region("uc", [P, 3], F32)
        tg, _ = region("tg", [P, 2], F32)
        graw, _ = region("graw", [P, 2], F32)
        cmax, _ = region("cmax", [P, 2, NCH], F32)
        nmax, _ = region("nmax", [P, TT], F32)
        sums, _ = region("sums", [P, TT, 2], F32)
        tot, _ = region("tot", [P, TT], F32)
        rec, _ = region("rec", [P, TT], F32)
        gain, _ = region("gain", [P, TT], F32)
        r_next, _ = region("r_next", [P, TT], F32)
        r_now, _ = region("r_now", [P, TT], F32)
        stats, _ = region("stats", [P, TT, 6], F32)
        mv, _ = region("mv", [P, TT, 2], F32)
        var, _ = region("var", [P, TT], F32)
        scaled, _ = region("scaled", [P, 2, TT], F32)
        rs, _ = region("rs", [P, TT], F32)
        rt, _ = region("rt", [P, TT], F32)
        wsum, _ = region("wsum", [P, 2], F32)
        thr, _ = region("thr", [P, 2], F32)
        gate, _ = region("gate", [P, NS + 6], F32)
        pgate, _ = region("pgate", [P, 2], F32)
        ones, _ = region("ones", [P, P], F32)
        assert place[0] <= nc.sbuf_usable_end, place[0]
        mask_i = alias("mask_i", [P, TT, KEYS], I32, pt_at)
        wraw = alias("wraw", [P, 4, DC, D], F32, w2T_at)
        wT = alias("wT", [P, 3, DC, D], F32, w1T_at)
        rep = alias("rep", [P, 2, DC, P], F32, w1T_at + 3 * DC * D * 4)
        w1abs = alias("w1abs", [P, FT, D], F32, pt_lo_at)
        tmp = alias("tmp", [P, 2 * TOK], F32, tmp_at)
        hid_at = tmp_at + 2 * TOK * 4
        w1raw = alias("w1raw", [P, FT, D], F32, hid_at)
        w2raw = alias("w2raw", [P, DC, FF], F32, hid_at)

        s_ps = [stack.enter_context(nc.psum_tensor(f"s_ps{i}", [P, 512], F32)) for i in range(SB)]
        e_ps = [stack.enter_context(nc.psum_tensor(f"e_ps{i}", [P, 512], F32)) for i in range(EB)]
        acc = [stack.enter_context(nc.psum_tensor(f"acc{i}", [P, 512], F32)) for i in range(2)]

        e_full, e_hi, e_free = sem("e_full"), sem("e_hi"), sem("e_free")
        s_full, s_biased, s_masked = sem("s_full"), sem("s_biased"), sem("s_masked")
        max_ready, exp_done = sem("max_ready"), sem("exp_done")
        pv_full, attn_hi, attn_split = sem("pv_full"), sem("attn_hi"), sem("attn_split")
        y_full, y_taken = sem("y_full"), sem("y_taken")
        xn_ready, xn2_ready, r_ready = sem("xn_ready"), sem("xn2_ready"), sem("r_ready")
        xl_loaded, xr_loaded, raw_loaded = sem("xl_loaded"), sem("xr_loaded"), sem("raw_loaded")
        xb_ready, x1b_ready = sem("xb_ready"), sem("x1b_ready")
        c_split, dve_step = sem("c_split"), sem("dve_step")
        qk_loaded, vo_loaded, bias_loaded = sem("qk_loaded"), sem("vo_loaded"), sem("bias_loaded")
        qk_bias_loaded = sem("qk_bias_loaded")
        mask_loaded = [sem(f"mask_loaded{t}") for t in range(TT)]
        mask_ready = sem("mask_ready")
        w1_loaded, w2_loaded, gate_ready = sem("w1_loaded"), sem("w2_loaded"), sem("gate_ready")
        const_ready, ident_zero = sem("const_ready"), sem("ident_zero")
        tern_above = sem("tern_above")
        tern_minus, tern_sum, tern = sem("tern_minus"), sem("tern_sum"), sem("tern")
        h_hi, c_hi_ready = sem("h_hi"), sem("c_hi_ready")
        wsum_ready, rep_ready = sem("wsum_ready"), sem("rep_ready")
        out_stored = sem("out_stored")

        xv = x.rearrange("b (t p) d -> b p t d", p=P)
        ov = out.rearrange("b (t p) d -> b p t d", p=P)
        cfull = ctx_in[:, 0:(KT - 1) * P, :].rearrange("b (t p) d -> b p t d", p=P)
        crem = ctx_in[:, (KT - 1) * P:KEYS, :]

        def of(ap, b, pat):
            return ap[bass.ds(b, 1)].rearrange(pat)

        def f32(ap):
            return ap.bitcast(F32)

        def key_tiles(piece):
            return slice(4 * piece, min(4 * piece + 4, KT)), P if piece < 3 else KREM

        def weight_half(h):
            if h < 2:
                return w1raw[:, 4 * h:4 * h + 4, :], tmp[:].rearrange("p (f d) -> p f d", d=D)
            return (w2raw[:, :, (h - 2) * 512:(h - 1) * 512],
                    tmp[:].rearrange("p (c f) -> p c f", c=DC))

        block = stack.enter_context(nc.Block())

        @block.sync
        def _(sp):
            def load_x(dst, b, done):
                sp.dma_start(dst[:], of(xv, b, "b p t d -> (b p) t d")).then_inc(done, 16)

            def load_context(b):
                sp.dma_start(raw[:, 0:KT - 1, :],
                             of(cfull, b, "b p t d -> (b p) t d")).then_inc(raw_loaded, 16)
                sp.dma_start(raw[0:KREM, KT - 1, :],
                             of(crem, b, "b p d -> (b p) d")).then_inc(raw_loaded, 16)

            def load_weight(i, w, done):
                sp.dma_start(wraw[:, i, :, :], w.rearrange("(c p) n -> p c n", p=P)
                             ).then_inc(done, 16)

            def load_column(dst, src, done):
                sp.dma_start(dst[:], src.rearrange("(c p) -> p c", p=P),
                             allow_slow_non_contiguous=True).then_inc(done, 16)

            load_weight(0, Wq, qk_loaded)
            load_weight(1, Wk, qk_loaded)
            load_x(xl, 0, xl_loaded)
            load_column(bkc, bk, qk_bias_loaded)
            load_column(bqc, bq, qk_bias_loaded)
            load_context(0)
            for t in range(TT):
                sp.dma_start(mask_i[:, t, :], mask[t * P:(t + 1) * P, :]
                             ).then_inc(mask_loaded[t], 16)
                if t == 1:
                    for i, g in enumerate((g_x, g_f)):
                        sp.dma_start(graw[:, i:i + 1], g.partition_broadcast(P)
                                     ).then_inc(bias_loaded, 16)
                    load_column(bvc, bv, bias_loaded)
                    load_weight(2, Wv, vo_loaded)
                    load_weight(3, Wo, vo_loaded)
                    for dst, src in ((tb1, bo), (tb2, b2)):
                        sp.dma_start(dst[:], src.partition_broadcast(P)).then_inc(bias_loaded, 16)
                    load_column(b1c, b1, bias_loaded)
                if t == 2:
                    sp.dma_start(w1raw[:], W1.rearrange("(t p) d -> p t d", p=P)
                                 ).then_inc(w1_loaded, 16)

            def batch(b):
                at = Batch(b)
                if not at.last:
                    if at.first:
                        sp.wait_ge(r_ready, 1)
                    else:
                        sp.wait_ge(e_full, at.base(len(MID), len(FIRST), len(PRO)))
                    load_x(xl, b + 1, xl_loaded)
                if not at.first:
                    sp.wait_ge(out_stored, b * (16 * 2))
                load_x(xr, b, xr_loaded)
                if not at.last:
                    sp.wait_ge(c_split, 4 * b + 4)
                    if at.first:
                        sp.wait_ge(e_full, len(PRO))
                    load_context(b + 1)
                if at.first:
                    sp.wait_ge(e_full, at.use("A3") + 1)
                    sp.dma_start(w2raw[:], W2.rearrange("(c p) f -> p c f", p=P)
                                 ).then_inc(w2_loaded, 16)
                for h in range(2):
                    sp.wait_ge(y_taken, b * TT + 2 * h + 2)
                    sp.dma_start(of(ov, b, "b p t d -> (b p) t d")[:, 2 * h:2 * h + 2, :],
                                 xr[:, 2 * h:2 * h + 2, :]).then_inc(out_stored, 16)

            batch(0)
            with sp.Fori(1, BATCH - 1) as b:
                batch(b)
            batch(BATCH - 1)
            sp.wait_ge(out_stored, BATCH * 2 * 16)

        @block.gpsimd
        def _(pool):
            nc.gpsimd.memset(ident[:], 0.0).then_inc(ident_zero, 1)
            nc.gpsimd.memset(ones[:], 1.0).then_inc(const_ready, 1)
            nc.gpsimd.memset(pgate[:], 0.0).then_inc(const_ready, 1)
            nc.gpsimd.memset(f32(cT_hi[:, :, KEYS:KEYS2]), 0.0).then_inc(const_ready, 1)
            nc.gpsimd.memset(f32(cT_lo[:, :, KEYS:KEYS2]), 0.0).then_inc(const_ready, 1)
            pool.wait_ge(ident_zero, 1)
            nc.gpsimd.affine_select(out=ident[:], in_=ident[:], compare_op=ALU.not_equal, fill=1.0,
                                    base=0, pattern=[[-1, P]],
                                    channel_multiplier=1).then_inc(const_ready, 1)
            pool.wait_ge(const_ready, 5)

            def split_context(b):
                for piece in range(4):
                    k, n = key_tiles(piece)
                    pool.wait_ge(c_hi_ready, 4 * b + (piece + 1))
                    nc.gpsimd.tensor_tensor(c_lo[0:n, k, :], raw[0:n, k, :], f32(c_hi[0:n, k, :]),
                                            ALU.subtract).then_inc(c_split, 1)

            def ternarise(half):
                w, t = weight_half(half)
                pool.wait_ge(tern_minus, half + 1)
                nc.gpsimd.tensor_tensor(t, t, w, ALU.add).then_inc(tern_sum, 1)
                pool.wait_ge(tern_sum, half + 1)
                nc.gpsimd.tensor_tensor(w, w, t, ALU.subtract).then_inc(tern, 1)

            def batch(b):
                at = Batch(b)
                split_context(b)
                if at.first:
                    for half in range(4):
                        ternarise(half)
                pool.wait_ge(e_free, PRO.index("bvo") + 1)
                pool.wait_ge(xr_loaded, 16 * b + 16)
                for t in range(TT):
                    ins = nc.gpsimd.tensor_tensor(xr[:, t, :], xr[:, t, :], tb1[:], ALU.add)
                ins.then_inc(xb_ready, 1)
                for h in range(2):
                    pool.wait_ge(xn2_ready, 2 * b + (h + 1))
                    for t in range(2 * h, 2 * h + 2):
                        ins = nc.gpsimd.tensor_tensor(xr[:, t, :], xr[:, t, :], tb2[:], ALU.add)
                    ins.then_inc(x1b_ready, 1)

            pool.wait_ge(raw_loaded, 32)
            for piece in range(4):
                k, n = key_tiles(piece)
                nc.gpsimd.tensor_copy(c_hi[0:n, k, :], raw[0:n, k, :]).then_inc(c_hi_ready, 1)
            batch(0)
            with pool.Fori(1, BATCH - 1) as b:
                batch(b)
            batch(BATCH - 1)

        @block.tensor
        def _(pe):
            def begin(count, name, bank):
                if isinstance(count, int) and count < EB:
                    return e_ps[bank]
                pe.wait_ge(e_free, count + (1 - EB))
                return e_ps[bank]

            def turn(out_, in_, n):
                return nc.tensor.transpose(out_, in_, ident[0:n, 0:n])

            def split_product(ps, parts, start, stop):
                for i, (l, r) in enumerate(parts):
                    ins = nc.tensor.matmul(ps, l, r, start=start and i == 0,
                                           stop=stop and i == len(parts) - 1)
                return ins

            def scores(b, n):
                t, c = divmod(n, NCH)
                if not (isinstance(b, int) and b == 0 and n < SB):
                    pe.wait_ge(s_masked, b * NS + (n - SB + 1))
                if t == 0:
                    g = min((CEND[c] - 1) // 512, 3)
                    if isinstance(b, int) and b == 0:
                        pe.wait_ge(e_free, max(PRO.index(f"C{2 * g + 1}"), PRO.index("Q1")) + 1)
                        pe.wait_ge(const_ready, 5)
                    else:
                        pe.wait_ge(e_free, Batch(b - 1).use_of_last(f"C{2 * g + 1}", "Q1") + 1)
                parts = []
                for d in range(DC):
                    q = slice(t * P, (t + 1) * P)
                    k = slice(CSTART[c], CEND[c])
                    parts += [(qT_hi[:, d, q], cT_hi[:, d, k]), (qT_lo[:, d, q], cT_hi[:, d, k]),
                              (qT_hi[:, d, q], cT_lo[:, d, k])]
                split_product(s_ps[c % SB][:, 0:CEND[c] - CSTART[c]], parts, True, True
                              ).then_inc(s_full, 1)

            def exchange(count, name, bank, b):
                kind, i = name[0], int(name[1:]) if name[1:].isdigit() else 0
                ps = begin(count, name, bank)
                if kind == "T":
                    t, c = divmod(i, 4)
                    pe.wait_ge(exp_done, 2 * TT * b + (2 * t + c // 2 + 1))
                    for j, k in enumerate(range(4 * c, min(4 * c + 4, KT))):
                        n = min(P, KEYS - k * P)
                        ins = turn(ps[0:n, j * P:(j + 1) * P],
                                   probs[:, t % 2, k * P:k * P + n], P)
                elif kind == "X":
                    pe.wait_ge(xn_ready, b + 1)
                    for t in range(TT):
                        ins = turn(ps[:, t * P:(t + 1) * P], xl[:, t, i * P:(i + 1) * P], P)
                elif kind == "Y":
                    pe.wait_ge(xn2_ready, 2 * b + (i + 1))
                    for d in range(DC):
                        for j in range(2):
                            ins = turn(ps[:, (2 * d + j) * P:(2 * d + j + 1) * P],
                                       xn2[:, 2 * i + j, d * P:(d + 1) * P], P)
                elif kind == "C":
                    g, d = divmod(i, DC)
                    pe.wait_ge(raw_loaded, 32 * b + 32)
                    for j, k in enumerate(range(4 * g, min(4 * g + 4, KT))):
                        n = min(P, KEYS - k * P)
                        ins = turn(ps[:, j * P:j * P + n], raw[0:n, k, d * P:(d + 1) * P], n)
                elif kind == "Q":
                    if isinstance(b, int) and b == 0:
                        pe.wait_ge(e_free, PRO.index("X1") + 1)
                    else:
                        pe.wait_ge(e_free, Batch(b - 1).use("X1") + 1)
                    parts = []
                    for d in range(DC):
                        m = slice(i * P, (i + 1) * P)
                        parts += [(m_hi[:, d, m], xT_hi[:, d, :]), (m_hi[:, d, m], xT_lo[:, d, :]),
                                  (m_lo[:, d, m], xT_hi[:, d, :])]
                    ins = split_product(ps[:], parts, True, True)
                elif kind == "O":
                    pe.wait_ge(attn_split, 2 * b + (i + 1))
                    for j in range(2):
                        q = slice((2 * i + j) * P, (2 * i + j + 1) * P)
                        parts = []
                        for d in range(DC):
                            parts += [(pt_hi[:, FT + d, q], vo_hi[:, d, :]),
                                      (pt_lo[:, FT + d, q], vo_hi[:, d, :]),
                                      (pt_hi[:, FT + d, q], vo_lo[:, d, :])]
                        ins = split_product(ps[:, j * D:(j + 1) * D], parts, True, True)
                elif kind == "H":
                    h, g = divmod(i, 4)
                    if g == 0:
                        pe.wait_ge(e_free, Batch(b).use(f"Y{h}") + 1)
                    q = slice(2 * h * P, 2 * (h + 1) * P)
                    for j in range(2):
                        parts = []
                        for d in range(DC):
                            w = w1T[:, d, (2 * g + j) * P:(2 * g + j + 1) * P]
                            parts += [(w, xT_hi[:, d, q]), (w, xT_lo[:, d, q])]
                        ins = split_product(ps[:, j * D:(j + 1) * D], parts, True, True)
                elif name in ("WqT", "WkT", "WvT"):
                    w = ("WqT", "WkT", "WvT").index(name)
                    pe.wait_ge(vo_loaded if w == 2 else qk_loaded, 32)
                    for e in range(DC):
                        for r in range(DC):
                            ins = turn(ps[:, e * D + r * P:e * D + (r + 1) * P],
                                       wraw[:, w, r, e * P:(e + 1) * P], P)
                elif name in ("M", "Wvo"):
                    pe.wait_ge(e_free, count)
                    w = 0 if name == "M" else 2
                    for r in range(DC):
                        for e in range(DC):
                            right = wT[:, 1, e, :] if name == "M" else wraw[:, 3, e, :]
                            ins = nc.tensor.matmul(ps[:, r * D:(r + 1) * D],
                                                   wT[:, w, e, r * P:(r + 1) * P], right,
                                                   start=e == 0, stop=e == DC - 1)
                elif name == "UC":
                    pe.wait_ge(rep_ready, 1)
                    for col, w, left, right in (
                            (0, D, lambda e: rep[:, 0, e, :], lambda e: wT[:, 0, e, :]),
                            (D, 1, lambda e: rep[:, 0, e, :], lambda e: bqc[:, e:e + 1]),
                            (D + 1, 1, lambda e: wT[:, 1, e, 0:P], lambda e: bqc[:, e:e + 1]),
                            (D + 2, 1, lambda e: wT[:, 1, e, P:D], lambda e: bqc[:, e:e + 1])):
                        for e in range(DC):
                            ins = nc.tensor.matmul(ps[:, col:col + w], left(e), right(e),
                                                   start=e == 0, stop=e == DC - 1)
                elif name == "bvo":
                    pe.wait_ge(rep_ready, 2)
                    for e in range(DC):
                        ins = nc.tensor.matmul(ps[:, 0:D], rep[:, 1, e, :], wraw[:, 3, e, :],
                                               start=e == 0, stop=e == DC - 1)
                elif kind == "S":
                    pe.wait_ge(wsum_ready, 1 if i == 1 else 3)
                    for j in range(i):
                        ins = nc.tensor.matmul(ps[:, 0:1], ones[:], wsum[:, j:j + 1],
                                               start=j == 0, stop=j == i - 1)
                elif kind == "A":
                    pe.wait_ge(tern, i // 2 + 1)
                    for f in range(4):
                        ins = turn(ps[:, f * P:(f + 1) * P],
                                   w1raw[:, 4 * (i // 2) + f, (i % 2) * P:(i % 2 + 1) * P], P)
                elif kind == "B":
                    pe.wait_ge(tern, 2 + i // 2 + 1)
                    for f in range(2):
                        for d in range(DC):
                            at = (2 * i + f) * P
                            ins = turn(ps[:, f * D + d * P:f * D + (d + 1) * P],
                                       w2raw[:, d, at:at + P], P)
                ins.then_inc(e_full, 1)

            def prologue():
                pe.wait_ge(const_ready, 5)
                for i, name in enumerate(PRO):
                    exchange(i, name, i % EB, 0)
                    for n in PRO_SCORES.get(name, []):
                        scores(0, n)

            def one(at, name):
                b = at.b + 1 if name[0] in "XQC" else at.b
                exchange(at.use(name), name, at.bank(name), b)

            def attend(at, h):
                if not at.first:
                    pe.wait_ge(y_taken, (at.b - 1) * TT + (2 * h + 2))
                q = slice(2 * h * P, 2 * (h + 1) * P)
                for k in range(KT):
                    if k % 4 == 0:
                        pe.wait_ge(c_split, 4 * at.b + (k // 4 + 1))
                        pe.wait_ge(e_free, at.use(f"T{8 * h + 4 + k // 4}") + 1)
                    n = min(P, KEYS - k * P)
                    for d in range(DC):
                        w = slice(d * P, (d + 1) * P)
                        parts = [(c_hi[0:n, k, w], pt_hi[0:n, k, q]),
                                 (c_hi[0:n, k, w], pt_lo[0:n, k, q]),
                                 (c_lo[0:n, k, w], pt_hi[0:n, k, q])]
                        for i, (l, r) in enumerate(parts):
                            ins = nc.tensor.matmul(acc[h][:, d * D:(d + 1) * D], l, r,
                                                   start=k == 0 and d == 0 and i == 0,
                                                   stop=k == KT - 1 and d == DC - 1 and i == 2,
                                                   skip_group_check=True)
                    if k == KT - 1:
                        ins.then_inc(pv_full, 1)
                    for name in at.plan["key"][h][k]:
                        step(at, name)

            def step(at, name):
                if name[0] == "N":
                    scores(at.b + 1, int(name[1:]))
                elif name[0] == "F":
                    second_product(at, int(name[1:]))
                else:
                    one(at, name)

            def second_product(at, i):
                h, g = divmod(i, 4)
                pe.wait_ge(e_free, at.use(f"H{i}") + 1)
                for f in (2 * g, 2 * g + 1):
                    for t in (2 * h, 2 * h + 1):
                        q = slice(t * P, (t + 1) * P)
                        for j, part in enumerate((pt_hi, pt_lo)):
                            ins = nc.tensor.matmul(acc[h][:, (t % 2) * D:(t % 2 + 1) * D],
                                                   part[:, f, q], w2T[:, f, :],
                                                   start=f == 0 and t % 2 == 0 and j == 0,
                                                   stop=f == FT - 1 and t % 2 == 1 and j == 1,
                                                   skip_group_check=True)
                if g == 3:
                    ins.then_inc(y_full, 1)

            def batch(b):
                at = Batch(b)
                for n in range(AHEAD, NS):
                    for name in at.plan["score"][n]:
                        one(at, name)
                    scores(b, n)
                attend(at, 0)
                attend(at, 1)
                for name in at.plan["tail"]:
                    step(at, name)

            prologue()
            batch(0)
            with pe.Fori(1, BATCH - 1) as b:
                batch(b)
            batch(BATCH - 1)

        def shape_of(name):
            kind, i = name[0], int(name[1:]) if name[1:].isdigit() else 0
            if kind == "T":
                t, c = divmod(i, 4)
                n = min(4, KT - 4 * c)
                rows = P if c < 3 else KREM
                return ((pt_hi, pt_lo), rows,
                        lambda a: a[0:rows, 4 * c:4 * c + n, t * P:(t + 1) * P], n * P, n)
            if kind == "X":
                return (xT_hi, xT_lo), P, lambda a: a[:, i, :], TOK, 1
            if kind == "Y":
                return ((xT_hi, xT_lo), P, lambda a: a[:, :, 2 * i * P:2 * (i + 1) * P],
                        TOK, DC)
            if kind == "Q":
                return (qT_hi, qT_lo), P, lambda a: a[:, i, :], TOK, 1
            if kind == "C":
                g, d = divmod(i, DC)
                w = min(512, KEYS - 512 * g)
                return (cT_hi, cT_lo), P, lambda a: a[:, d, 512 * g:512 * g + w], w, 1
            if name == "M":
                return (m_hi, m_lo), P, lambda a: a[:], DC * D, DC
            if name == "Wvo":
                return (vo_hi, vo_lo), P, lambda a: a[:], DC * D, DC

        def psum_view(bank, rows, width, parts):
            v = e_ps[bank][0:rows, 0:width]
            return v.rearrange("p (a n) -> p a n", a=parts) if parts > 1 else v

        @block.scalar
        def _(act):
            def high(count, name, bank, b):
                (dst, _), rows, pick, width, parts = shape_of(name)
                act.wait_ge(e_full, count + 1)
                bias, scale = 0.0, 1.0
                if name[0] == "Q":
                    i = int(name[1])
                    bias = uc[:, 1 + i:2 + i]
                if name == "M":
                    scale = SCALE
                nc.scalar.activation(pick(dst), psum_view(bank, rows, width, parts),
                                     ACT.Identity, bias=bias, scale=scale).then_inc(e_hi, 1)

            def one(at, name):
                if not by_act(name):
                    return
                b = at.b + 1 if name[0] in "XQC" else at.b
                high(at.use(name), name, at.bank(name), b)

            def add_r(b, n):
                t, c = divmod(n, NCH)
                if n == 0:
                    act.wait_ge(r_ready, b + 1)
                act.wait_ge(s_full, b * NS + (n + 1))
                w = CEND[c] - CSTART[c]
                nc.scalar.activation(s_ps[c % SB][:, 0:w], s_ps[c % SB][:, 0:w], ACT.Identity,
                                     bias=r_now[:, t:t + 1]).then_inc(s_biased, 1)

            def exps(b, t, h):
                if h == 0:
                    act.wait_ge(max_ready, b * TT + (t + 1))
                v = probs[:, t % 2, 0:HALF] if h == 0 else probs[:, t % 2, HALF:KEYS]
                nc.scalar.activation(v, v, ACT.Exp, bias=nmax[:, t:t + 1],
                                     accum_out=sums[:, t, h:h + 1]).then_inc(exp_done, 1)

            def context_high(b, piece):
                if piece == 0:
                    act.wait_ge(raw_loaded, 32 * b + 32)
                k, n = key_tiles(piece)
                nc.scalar.activation(c_hi[0:n, k, :], raw[0:n, k, :],
                                     ACT.Identity).then_inc(c_hi_ready, 1)

            def sum_of_w1():
                act.wait_ge(w1_loaded, 16)
                nc.scalar.activation(w1abs[:], w1raw[:], ACT.Abs,
                                     accum_out=wsum[:, 0:1]).then_inc(wsum_ready, 1)

            def attention_high(b, h):
                act.wait_ge(pv_full, 2 * b + (h + 1))
                nc.scalar.activation(pt_hi[:, FT:FT + DC, 2 * h * P:2 * (h + 1) * P],
                                     acc[h][:].rearrange("p (d q) -> p d q", d=DC),
                                     ACT.Identity).then_inc(attn_hi, 1)

            def hidden(at, i):
                name = f"H{i}"
                act.wait_ge(e_full, at.use(name) + 1)
                if i >= 4:
                    act.wait_ge(e_free, at.use(f"H{i - 4}") + 1)
                for j in range(2):
                    f = 2 * (i % 4) + j
                    ins = nc.scalar.activation(hid[:, i % 4, j * D:(j + 1) * D],
                                               e_ps[at.bank(name)][:, j * D:(j + 1) * D],
                                               ACT.Gelu, bias=b1c[:, f:f + 1])
                ins.then_inc(e_hi, 1)

            def batch(b):
                at = Batch(b)
                exps(b, 1, 0)
                exps(b, 1, 1)
                if at.first:
                    act.wait_ge(mask_ready, TT)
                for n in range(AHEAD, NS):
                    for name in at.plan["score"][n]:
                        one(at, name)
                    add_r(b, n)
                    for share in range(2):
                        if n == EXP_AT[2][share]:
                            exps(b, 2, share)
                for h in range(2):
                    for k in range(KT):
                        if h == 0 and k in EXP_AT[3]:
                            exps(b, 3, EXP_AT[3].index(k))
                        if h == 1 and k == 0:
                            attention_high(b, 0)
                        for name in at.plan["key"][h][k]:
                            step(at, name)
                        if h == 1 and k in EXP_AT[0] and not at.last:
                            exps(b + 1, 0, EXP_AT[0].index(k))
                attention_high(b, 1)
                for name in at.plan["tail"]:
                    step(at, name)
                    if name in EXP_AT[0] and not at.last:
                        exps(b + 1, 0, EXP_AT[0].index(name))
                    if name in ROUND_AT and not at.last:
                        context_high(b + 1, ROUND_AT.index(name))

            def step(at, name):
                if name[0] == "N":
                    add_r(at.b + 1, int(name[1:]))
                elif name[0] == "H":
                    hidden(at, int(name[1:]))
                elif name[0] != "F":
                    one(at, name)

            for i, name in enumerate(PRO):
                if name == "Q0":
                    act.wait_ge(e_free, PRO.index("UC") + 1)
                if by_act(name):
                    high(i, name, i % EB, 0)
                for n in PRO_SCORES.get(name, []):
                    add_r(0, n)
                    if n == 1:
                        sum_of_w1()
                    if n == NCH:
                        exps(0, 0, 0)
                        exps(0, 0, 1)
                if name == "WvT":
                    act.wait_ge(bias_loaded, 6 * 16)
                    nc.scalar.activation(tg[:], graw[:], ACT.Tanh).then_inc(gate_ready, 1)
            batch(0)
            with act.Fori(1, BATCH - 1) as b:
                batch(b)
            batch(BATCH - 1)

        @block.vector
        def _(dve):
            step = {"base": 0, "n": 0}

            def link(ins):
                step["n"] += 1
                ins.then_inc(dve_step, 1)
                dve.wait_ge(dve_step, step["base"] + step["n"])

            def pin(i):
                nc.vector.memset(gate[:, i:i + 1], 0.0)

            def low(count, hi_count, name, bank, b):
                (dhi, dlo), rows, pick, width, parts = shape_of(name)
                dve.wait_ge(e_hi, hi_count + 1)
                ps, hi = psum_view(bank, rows, width, parts), f32(pick(dhi))
                if name[0] == "Q" or name == "M":
                    i = int(name[1]) if name[0] == "Q" else 0
                    ins = nc.vector.scalar_tensor_tensor(
                        out=pick(dlo), in0=ps, in1=hi, op1=ALU.subtract,
                        scalar=uc[:, 1 + i:2 + i] if name[0] == "Q" else SCALE,
                        op0=ALU.add if name[0] == "Q" else ALU.mult)
                else:
                    ins = nc.vector.tensor_tensor(pick(dlo), ps, hi, ALU.subtract)
                ins.then_inc(e_free, 1)

            def take(count, name, bank):
                kind, i = name[0], int(name[1:]) if name[1:].isdigit() else 0
                dve.wait_ge(e_full, count + 1)
                ps = e_ps[bank]
                if name in ("WqT", "WkT", "WvT"):
                    w = ("WqT", "WkT", "WvT").index(name)
                    ins = nc.vector.tensor_copy(
                        wT[:, w, :, :], ps[:].rearrange("p (e r) -> p e r", e=DC))
                elif name == "UC":
                    nc.vector.tensor_copy(U[:], ps[:, 0:D])
                    ins = nc.vector.tensor_scalar(uc[:], ps[:, D:D + 3], SCALE, None, ALU.mult)
                elif name == "bvo":
                    dve.wait_ge(gate_ready, 1)
                    link(nc.vector.tensor_tensor(tb1[:], ps[:, 0:D], tb1[:], ALU.add))
                    nc.vector.tensor_scalar(tb1[:], tb1[:], tg[:, 0:1], None, ALU.mult)
                    ins = nc.vector.tensor_scalar(tb2[:], tb2[:], tg[:, 1:2], None, ALU.mult)
                elif kind == "S":
                    link(nc.vector.tensor_scalar(wsum[:, 0:1], ps[:, 0:1], 1.0 / (FF * D), 1e-8,
                                                 ALU.mult, ALU.max))
                    nc.vector.tensor_scalar(thr[:, 0:1], wsum[:, 0:1], 0.5, None, ALU.mult)
                    ins = nc.vector.tensor_scalar(thr[:, 1:2], wsum[:, 0:1], -0.5, None, ALU.mult)
                elif kind == "A":
                    ins = nc.vector.tensor_copy(w1T[:, i % 2, (i // 2) * 512:(i // 2 + 1) * 512],
                                                ps[:])
                elif kind == "B":
                    ins = nc.vector.tensor_copy(w2T[:, 2 * i:2 * i + 2, :],
                                                ps[:].rearrange("p (f d) -> p f d", f=2))
                ins.then_inc(e_free, 1)

            def one(at, name):
                if by_act(name):
                    b = at.b + 1 if name[0] in "XQC" else at.b
                    low(at.use(name), at.hi(name), name, at.bank(name), b)
                else:
                    take(at.use(name), name, at.bank(name))

            def mask_scores(b, n):
                t, c = divmod(n, NCH)
                dve.wait_ge(s_biased, b * NS + (n + 1))
                pin(n)
                w = min(CEND[c], KEYS) - CSTART[c]
                k = slice(CSTART[c], CSTART[c] + w)
                nc.vector.tensor_tensor_reduce(probs[:, t % 2, k], s_ps[c % SB][:, 0:w], mbias[:, t, k],
                                               1.0, MASKED, ALU.add, ALU.max,
                                               cmax[:, t % 2, c:c + 1]).then_inc(s_masked, 1)
                if c == NCH - 1:
                    dve.wait_ge(s_masked, b * NS + (n + 1))
                    nc.vector.tensor_reduce(nmax[:, t:t + 1], cmax[:, t % 2, :], AX.X, ALU.max,
                                            negate=True).then_inc(max_ready, 1)

            def tile_stats(src, t):
                return nc.vector.bn_stats(stats[:, t, :], src[:, t, :])

            def ln_aggregate(src, first, end):
                pin(NS if src is xl else NS + 1 + first // 2)
                for t in range(first, end):
                    ins = nc.vector.bn_aggr(mv[:, t, :], stats[:, t, :])
                link(ins)

            def ln_stats(src, first=0, end=TT):
                for t in range(first, end):
                    ins = tile_stats(src, t)
                link(ins)
                ln_aggregate(src, first, end)

            def ln_seed():
                link(nc.vector.tensor_scalar(var[:], mv[:, :, 1], EPS, None, ALU.add))
                nc.vector.tensor_scalar(scaled[:, 0, :], var[:], NEWTON_W, None, ALU.mult)
                nc.vector.tensor_scalar(scaled[:, 1, :], var[:], HALLEY_W, None, ALU.mult)
                link(nc.vector.tensor_scalar(rt[:].bitcast(I32), var[:].bitcast(I32), 1, None,
                                             ALU.logical_shift_right))
                link(nc.vector.tensor_scalar(rs[:].bitcast(I32), rt[:].bitcast(I32), -1.0,
                                             float(RSQRT_SEED), ALU.mult, ALU.add))

            def ln_round(i):
                link(nc.vector.tensor_tensor(rt[:], rs[:], rs[:], ALU.mult))
                link(nc.vector.tensor_tensor(rt[:], rt[:], scaled[:, i, :], ALU.mult))
                if i == 0:
                    link(nc.vector.scalar_tensor_tensor(out=rs[:], in0=rt[:], scalar=NEWTON_C,
                                                        in1=rs[:], op0=ALU.add, op1=ALU.mult))
                else:
                    link(nc.vector.scalar_tensor_tensor(out=rt[:], in0=rt[:], scalar=HALLEY_B,
                                                        in1=rt[:], op0=ALU.add, op1=ALU.mult))
                    link(nc.vector.scalar_tensor_tensor(out=rs[:], in0=rt[:], scalar=HALLEY_C,
                                                        in1=rs[:], op0=ALU.add, op1=ALU.mult))

            def ln_apply(src, dst, done, first=0, end=TT):
                for t in range(first, end):
                    ins = nc.vector.tensor_scalar(dst[:, t, :], src[:, t, :], mv[:, t, 0:1],
                                                  rs[:, t:t + 1], ALU.subtract, ALU.mult)
                ins.then_inc(done, 1)

            def row_terms(b):
                dve.wait_ge(xn_ready, b + 1)
                pin(NS + 5)
                for t in range(TT):
                    ins = nc.vector.tensor_tensor_reduce(junk[:, t % 2, :], xl[:, t, :], U[:],
                                                         SCALE, uc[:, 0:1], ALU.mult, ALU.add,
                                                         r_next[:, t:t + 1])
                    if t % 2:
                        link(ins)
                        pin(NS + 3 + t // 2)

            def publish_r():
                nc.vector.tensor_copy(r_now[:], r_next[:]).then_inc(r_ready, 1)

            def rows_gain(b):
                dve.wait_ge(exp_done, 2 * TT * b + 2 * TT)
                link(nc.vector.tensor_tensor(tot[:], sums[:, :, 0], sums[:, :, 1], ALU.add))
                link(nc.vector.reciprocal(rec[:], tot[:]))
                link(nc.vector.tensor_scalar(gain[:], rec[:], tg[:, 0:1], None, ALU.mult))

            def attended(at, i):
                name = f"O{i}"
                if i == 0:
                    dve.wait_ge(xb_ready, at.b + 1)
                dve.wait_ge(e_full, at.use(name) + 1)
                for j in range(2):
                    t = 2 * i + j
                    ins = nc.vector.scalar_tensor_tensor(
                        out=xr[:, t, :], in0=e_ps[at.bank(name)][:, j * D:(j + 1) * D],
                        scalar=gain[:, t:t + 1], in1=xr[:, t, :], op0=ALU.mult, op1=ALU.add)
                ins.then_inc(e_free, 1)

            def mask_to_bias(t):
                dve.wait_ge(mask_loaded[t], 16)
                nc.vector.tensor_scalar(mbias[:, t, :], mask_i[:, t, :], 0, MASKED, ALU.is_equal,
                                        ALU.mult).then_inc(mask_ready, 1)

            def sum_of_w2(half):
                dve.wait_ge(w2_loaded, 16)
                nc.vector.tensor_reduce(wsum[:, half:half + 1], w2raw[:, half, :], AX.X, ALU.add,
                                        apply_absolute_value=True).then_inc(wsum_ready, 1)

            def ternary_above(h):
                w, t = weight_half(h)
                if h % 2 == 0:
                    dve.wait_ge(e_free, (PRO.index("S1") if h == 0 else Batch(0).use("S2")) + 1)
                if h > 0:
                    dve.wait_ge(tern, h)
                nc.vector.tensor_scalar(t, w, thr[:, 0:1], None, ALU.is_gt).then_inc(tern_above, 1)

            def ternary_below(h):
                w, t = weight_half(h)
                dve.wait_ge(tern_above, h + 1)
                nc.vector.scalar_tensor_tensor(out=t, in0=w, scalar=thr[:, 1:2], in1=t,
                                               op0=ALU.is_lt, op1=ALU.subtract
                                               ).then_inc(tern_minus, 1)

            def replicate(i, column):
                for e in range(DC):
                    ins = nc.vector.tensor_scalar(rep[:, i, e, :], ones[:], column[:, e:e + 1],
                                                  None, ALU.mult)
                ins.then_inc(rep_ready, 1)

            for i, name in enumerate(PRO):
                if by_act(name):
                    low(i, pro_hi(name), name, i % EB, 0)
                else:
                    take(i, name, i % EB)
                if name == "WkT":
                    dve.wait_ge(xl_loaded, 16)
                    ln_stats(xl)
                    dve.wait_ge(qk_bias_loaded, 32)
                    dve.wait_ge(const_ready, 5)
                    replicate(0, bkc)
                    ln_seed()
                    ln_round(0)
                    ln_round(1)
                    ln_apply(xl, xl, xn_ready)
                if name == "C1":
                    dve.wait_ge(e_free, PRO.index("UC") + 1)
                    row_terms(0)
                    publish_r()
                if name == "Q1":
                    mask_to_bias(0)
                for n in PRO_SCORES.get(name, []):
                    if n % NCH == 0:
                        dve.wait_ge(mask_ready, n // NCH + 1)
                    mask_scores(0, n)
                    if n == 0:
                        mask_to_bias(1)
                    if n in (3, 4):
                        mask_to_bias(n - 1)
                    if n == 6:
                        ternary_above(0)
                    if n == 7:
                        ternary_below(0)
                    if n == 5:
                        dve.wait_ge(bias_loaded, 6 * 16)
                        replicate(1, bvc)
            pro_steps = step["n"]

            def attention_low(b, h):
                q = slice(2 * h * P, 2 * (h + 1) * P)
                dve.wait_ge(attn_hi, 2 * b + (h + 1))
                nc.vector.tensor_tensor(pt_lo[:, FT:FT + DC, q],
                                        acc[h][:].rearrange("p (d q) -> p d q", d=DC),
                                        f32(pt_hi[:, FT:FT + DC, q]),
                                        ALU.subtract).then_inc(attn_split, 1)

            def hidden_parts(at, i):
                h, g = divmod(i, 4)
                src = hid[:, i % 4, :].rearrange("p (f q) -> p f q", f=2)
                dst = (slice(None), slice(2 * g, 2 * g + 2), slice(2 * h * P, 2 * (h + 1) * P))
                dve.wait_ge(e_hi, at.hi(f"H{i}") + 1)
                nc.vector.tensor_copy(pt_hi[dst], src).then_inc(h_hi, 1)
                dve.wait_ge(h_hi, at.b * 8 + (i + 1))
                nc.vector.tensor_tensor(pt_lo[dst], src, f32(pt_hi[dst]),
                                        ALU.subtract).then_inc(e_free, 1)

            def store_ready(at, h):
                dve.wait_ge(x1b_ready, 2 * at.b + (h + 1))
                dve.wait_ge(y_full, 2 * at.b + (h + 1))
                for t in (2 * h, 2 * h + 1):
                    nc.vector.scalar_tensor_tensor(
                        out=xr[:, t, :], in0=acc[h][:, (t % 2) * D:(t % 2 + 1) * D],
                        scalar=tg[:, 1:2], in1=xr[:, t, :], op0=ALU.mult,
                        op1=ALU.add).then_inc(y_taken, 1)

            def step_of(at, name):
                kind, i = name[0], int(name[1:])
                if kind == "N":
                    mask_scores(at.b + 1, i)
                elif kind == "H":
                    hidden_parts(at, i)
                elif kind == "O":
                    attended(at, i)
                elif kind != "F":
                    one(at, name)
                    if name == "Q1":
                        publish_r()
                elif i % 4 == 3:
                    store_ready(at, i // 4)

            def second_ln(at, h):
                def begin():
                    dve.wait_ge(e_free, at.use(f"O{h}") + 1)
                    ln_stats(xr, 2 * h, 2 * h + 2)

                def middle():
                    ln_seed()
                    ln_round(0)

                def rest():
                    ln_round(1)
                    ln_apply(xr, xn2, xn2_ready, 2 * h, 2 * h + 2)
                return [begin, middle, rest]

            def batch(b, base):
                at = Batch(b)
                step["base"], step["n"] = base, 0
                ln = {} if at.last else dict(zip(LN_AT, (
                    lambda: (dve.wait_ge(xl_loaded, 16 * b + 32), tile_stats(xl, 0)),
                    lambda: tile_stats(xl, 1), lambda: tile_stats(xl, 2),
                    lambda: link(tile_stats(xl, 3)), lambda: ln_aggregate(xl, 0, TT),
                    ln_seed, lambda: ln_round(0), lambda: ln_round(1),
                    lambda: ln_apply(xl, xl, xn_ready), lambda: row_terms(b + 1))))
                for n in range(AHEAD, NS):
                    for name in at.plan["score"][n]:
                        one(at, name)
                    if at.first and n % NCH == 0:
                        dve.wait_ge(mask_ready, n // NCH + 1)
                    mask_scores(b, n)
                    if at.first and n == TERN1_AT[0]:
                        ternary_above(1)
                    if at.first and n == TERN1_AT[1]:
                        ternary_below(1)
                    if n in ln:
                        ln[n]()
                for k in range(KT):
                    for name in at.plan["key"][0][k]:
                        one(at, name)
                    if NS + k in ln:
                        ln[NS + k]()
                    if at.first and k in W2_SUM_AT:
                        sum_of_w2(W2_SUM_AT.index(k))
                    if at.first and k == TERN2_AT[0]:
                        ternary_above(2)
                    if at.first and k == TERN2_AT[1]:
                        ternary_below(2)
                rows_gain(b)
                pieces = second_ln(at, 0)
                pieces_at = FIRST_LN2_KEY if at.first else LN2_KEY
                for k in range(KT):
                    if k == 0:
                        attention_low(b, 0)
                    for name in at.plan["key"][1][k]:
                        step_of(at, name)
                    if at.first and k == TERN3_AT[0]:
                        ternary_above(3)
                    if at.first and k == TERN3_AT[1]:
                        ternary_below(3)
                    for piece, place in zip(pieces, pieces_at):
                        if place == k:
                            piece()
                attention_low(b, 1)
                pieces = second_ln(at, 1)
                pieces_at = LAST_LN2_TAIL if at.last else LN2_TAIL
                for name in at.plan["tail"]:
                    step_of(at, name)
                    for piece, place in zip(pieces, pieces_at):
                        if place == name:
                            piece()
                return step["n"]

            n0 = batch(0, pro_steps)
            with dve.Fori(1, BATCH - 1) as b:
                n1 = batch(b, (b - 1) * BODY_STEPS + (pro_steps + n0))
            assert n1 == BODY_STEPS, n1
            batch(BATCH - 1, (BATCH - 2) * BODY_STEPS + pro_steps + n0)


_INS = ['x', 'ctx_1024', 'mask_SxS2_ik0', 'g_xattn', 'g_ffn', 'L0_xattn_Wq', 'L0_xattn_bq',
        'L0_xattn_Wk', 'L0_xattn_bk', 'L0_xattn_Wv', 'L0_xattn_bv', 'L0_xattn_Wo', 'L0_xattn_bo',
        'L0_ffn_W1', 'L0_ffn_b1', 'L0_ffn_W2', 'L0_ffn_b2']


def kernel(**inputs):
    import numpy as _np
    import concourse.bacc as _bacc
    from concourse import mybir as _mybir
    from concourse.bass_utils import run_bass_kernel_spmd as _run

    nc = _bacc.Bacc("TRN2", target_bir_lowering=False, num_devices=1)
    arrays, args = {}, []
    for name in _INS:
        a = _np.ascontiguousarray(inputs[name])
        arrays[f"in_{name}_dram"] = a
        args.append(nc.dram_tensor(f"in_{name}_dram", a.shape, _mybir.dt.from_np(a.dtype),
                                   kind="ExternalInput").ap())
    args.append(nc.dram_tensor("out_dram", (BATCH, TOK, D), _mybir.dt.float32,
                               kind="ExternalOutput").ap())
    build(nc, *args)
    r = _run(nc, [arrays], core_ids=[0])
    return r.results[0]["out_dram"]
```
